# Optimizing a Trainium2 kernel written in Bass

```python
import numpy as np
import jax
import jax.numpy as jnp

def _softmax(x, axis=-1):
    return jax.nn.softmax(x, axis=axis)

def _gelu(x):
    return jax.nn.gelu(x, approximate=True)

def _silu(x):
    return jax.nn.silu(x)

def _sigmoid(x):
    return jax.nn.sigmoid(x)

def _layernorm(x, axis=-1, eps=1e-05):
    m = jnp.mean(x, axis=axis, keepdims=True)
    v = jnp.var(x, axis=axis, keepdims=True)
    return (x - m) / jnp.sqrt(v + eps)

def _scatter_add(tgt, idx, src, axis=0):
    return tgt.at[idx].add(src)

def _segment_sum(src, seg, n):
    return jax.ops.segment_sum(src, seg, n)
kernel_name = 'mk_seq_postln_d1_jaxref_r8_995574'

def setup_inputs(seed: int=0):
    np.random.seed(seed)
    _w = jnp.asarray

    def _L0_attn_setup():
        import jax, jax.numpy as jnp
        import numpy as np
        B, S, DM = (2, 256, 256)
        H, KVH, HD = (16, 4, 128)
        REP = H // KVH
        ROPE_BASE = 10000.0
        EPS = 1e-06

        def _rope_tables(seq_len, dim):
            inv_freq = 1.0 / ROPE_BASE ** (jnp.arange(0, dim, 2, dtype=jnp.float32) / dim)
            t = jnp.arange(seq_len, dtype=jnp.float32)
            freqs = jnp.outer(t, inv_freq)
            emb = jnp.concatenate([freqs, freqs], -1)
            return (jnp.cos(emb), jnp.sin(emb))

        def _rotate_half(x):
            d = x.shape[-1] // 2
            return jnp.concatenate([-x[..., d:], x[..., :d]], axis=-1)
        key = jax.random.key(seed)
        k0, k1, k2, k3, k4 = jax.random.split(key, 5)
        w = lambda k, o, i: jax.random.normal(k, (o, i), jnp.float32) * (1.0 / np.sqrt(i))
        return {'x': jax.random.normal(k0, (B, S, DM), jnp.float32), 'Wq': w(k1, H * HD, DM), 'Wk': w(k2, KVH * HD, DM), 'Wv': w(k3, KVH * HD, DM), 'Wo': w(k4, DM, H * HD)}
    _L0_attn_in = _L0_attn_setup()

    def _L0_ffn_setup():
        import jax, jax.numpy as jnp
        import numpy as np
        D_MODEL = 256
        HIDDEN = int(2 * D_MODEL * 4 / 3)

        def ternary_quant(w):
            s = jnp.mean(jnp.abs(w))
            q = jnp.clip(jnp.round(w / s), -1.0, 1.0) * s
            return w + jax.lax.stop_gradient(q - w)
        key = jax.random.key(seed)
        k0, k1, k2, k3 = jax.random.split(key, 4)
        x = jax.random.normal(k0, (4, 512, D_MODEL), dtype=jnp.float32)
        std_in = 1.0 / np.sqrt(D_MODEL)
        std_h = 1.0 / np.sqrt(HIDDEN)
        w1 = jax.random.uniform(k1, (HIDDEN, D_MODEL), jnp.float32, -std_in, std_in)
        w3 = jax.random.uniform(k2, (HIDDEN, D_MODEL), jnp.float32, -std_in, std_in)
        w2 = jax.random.uniform(k3, (D_MODEL, HIDDEN), jnp.float32, -std_h, std_h)
        return {'x': x, 'w1': w1, 'w3': w3, 'w2': w2}
    _L0_ffn_in = _L0_ffn_setup()
    _d = {'L0_attn_x': _L0_attn_in['x'], 'L0_attn_Wq': _L0_attn_in['Wq'], 'L0_attn_Wk': _L0_attn_in['Wk'], 'L0_attn_Wv': _L0_attn_in['Wv'], 'L0_attn_Wo': _L0_attn_in['Wo'], 'L0_ffn_w1': _L0_ffn_in['w1'], 'L0_ffn_w3': _L0_ffn_in['w3'], 'L0_ffn_w2': _L0_ffn_in['w2']}
    _x0 = _d['L0_attn_x']
    _d['L0_attn_x'] = jax.random.normal(jax.random.fold_in(jax.random.key(seed), 1), (1, 1024, 256), dtype=_x0.dtype)
    del _x0
    return _d

def reference(L0_attn_x, L0_attn_Wq, L0_attn_Wk, L0_attn_Wv, L0_attn_Wo, L0_ffn_w1, L0_ffn_w3, L0_ffn_w2):

    def _L0_attn_ref(x, Wq, Wk, Wv, Wo):
        import jax, jax.numpy as jnp
        import numpy as np
        B, S, DM = (2, 256, 256)
        H, KVH, HD = (16, 4, 128)
        REP = H // KVH
        ROPE_BASE = 10000.0
        EPS = 1e-06

        def _rope_tables(seq_len, dim):
            inv_freq = 1.0 / ROPE_BASE ** (jnp.arange(0, dim, 2, dtype=jnp.float32) / dim)
            t = jnp.arange(seq_len, dtype=jnp.float32)
            freqs = jnp.outer(t, inv_freq)
            emb = jnp.concatenate([freqs, freqs], -1)
            return (jnp.cos(emb), jnp.sin(emb))

        def _rotate_half(x):
            d = x.shape[-1] // 2
            return jnp.concatenate([-x[..., d:], x[..., :d]], axis=-1)
        bsz, seq_len, _ = x.shape
        q = (x @ Wq.T).reshape(bsz, seq_len, H, HD).transpose(0, 2, 1, 3)
        k = (x @ Wk.T).reshape(bsz, seq_len, KVH, HD).transpose(0, 2, 1, 3)
        v = (x @ Wv.T).reshape(bsz, seq_len, KVH, HD).transpose(0, 2, 1, 3)
        cos, sin = _rope_tables(seq_len, HD)
        cos, sin = (cos[None, None], sin[None, None])
        q = q * cos + _rotate_half(q) * sin
        k = k * cos + _rotate_half(k) * sin
        k = jnp.repeat(k, REP, axis=1)
        v = jnp.repeat(v, REP, axis=1)
        qf = jax.nn.elu(q) + 1.0
        kf = jax.nn.elu(k) + 1.0
        qf_t = qf.transpose(2, 0, 1, 3)
        kf_t = kf.transpose(2, 0, 1, 3)
        v_t = v.transpose(2, 0, 1, 3)

        def step(carry, inp):
            state, z = carry
            q_s, k_s, v_s = inp
            state = state + k_s[..., :, None] * v_s[..., None, :]
            z = z + k_s
            num = jnp.einsum('bhe,bhed->bhd', q_s, state)
            den = jnp.einsum('bhe,bhe->bh', q_s, z)[..., None] + EPS
            return ((state, z), num / den)
        init = (jnp.zeros((bsz, H, HD, HD), x.dtype), jnp.zeros((bsz, H, HD), x.dtype))
        _, out = jax.lax.scan(step, init, (qf_t, kf_t, v_t))
        out = out.transpose(1, 0, 2, 3).reshape(bsz, seq_len, H * HD)
        return out @ Wo.T

    def _L0_ffn_ref(x, w1, w3, w2):
        import jax, jax.numpy as jnp
        import numpy as np
        D_MODEL = 256
        HIDDEN = int(2 * D_MODEL * 4 / 3)

        def ternary_quant(w):
            s = jnp.mean(jnp.abs(w))
            q = jnp.clip(jnp.round(w / s), -1.0, 1.0) * s
            return w + jax.lax.stop_gradient(q - w)
        w1q = ternary_quant(w1)
        w3q = ternary_quant(w3)
        w2q = ternary_quant(w2)
        h1 = jnp.einsum('bsd,hd->bsh', x, w1q)
        h3 = jnp.einsum('bsd,hd->bsh', x, w3q)
        g = jax.nn.silu(h1) * h3
        return jnp.einsum('bsh,dh->bsd', g, w2q)
    x = L0_attn_x
    x = _layernorm(x + _L0_attn_ref(x, L0_attn_Wq, L0_attn_Wk, L0_attn_Wv, L0_attn_Wo), axis=-1)
    x = _layernorm(x + _L0_ffn_ref(x, L0_ffn_w1, L0_ffn_w3, L0_ffn_w2), axis=-1)
    return x

_drawn_inputs = setup_inputs


def setup_inputs(seed=0):
    import zlib

    import numpy as np

    out = dict(_drawn_inputs(seed))
    spreads = {}
    factors = {}
    for name, (base, spread) in spreads.items():
        noise = np.random.default_rng([zlib.crc32(name.encode()), seed]).standard_normal(out[name].shape)
        drawn = base * np.exp(spread * noise) if base else spread * noise
        out[name] = jnp.asarray(drawn.astype(out[name].dtype))
    for name, factor in factors.items():
        out[name] = (out[name] * factor).astype(out[name].dtype)
    return out
```

```python
from contextlib import ExitStack

import numpy as np

import concourse.bass as bass
from concourse import mybir

P = 128
F32 = mybir.dt.float32
F32R = mybir.dt.float32r
ALU = mybir.AluOpType
ACT = mybir.ActivationFunctionType

S, DM = 1024, 256
HEADS, KV_HEADS, HD = 16, 4, 128
REP = HEADS // KV_HEADS
HIDDEN = int(2 * DM * 4 / 3)
ROPE_BASE = 10000.0
DEN_EPS = 1e-6
LN_EPS = 1e-5

CHUNKS = S // P
KT = DM // P
GROUPS = KV_HEADS
GW = REP * HD
VW = HD + 1
VS = HD + 2
HALF = HD // 2

HALVES = 2
HALF_S = S // HALVES
TILES = HALF_S // P
HC = -(-HIDDEN // P)
HW = HIDDEN // HC + 1
HID = [min(HW, HIDDEN - j * HW) for j in range(HC)]

LOOP = 4
FFN_LOOP = 12


class Stage:

    def __init__(self, sem, per, whole):
        self.sem, self.step, self.whole = sem, whole // per, whole

    def done(self, base, k=0):
        return base + self.whole + (k + 1) * self.step


def build(nc, x_seq, x_t, wq_t, wk_t, wv_t, wo_t, w1_t, w3_t, w2_t, tables, out):
    with ExitStack() as ctx:
        def sb(name, shape, dt=F32):
            return ctx.enter_context(nc.sbuf_tensor(name, shape, dt))

        def sem(name):
            return ctx.enter_context(nc.semaphore(name))

        def stage(name, per=1, whole=LOOP):
            return Stage(sem(name), per, whole)

        const = sb("const", [P, 2 * P + CHUNKS * (HALF + HD)])
        causal = const[:, 0:P]
        ident = const[:, P:2 * P]
        cos = const[:, 2 * P:2 * P + CHUNKS * HALF]
        sin = const[:, 2 * P + CHUNKS * HALF:]
        x_all = sb("x_all", [P, CHUNKS, DM])
        xt_all = sb("xt_all", [P, KT, S])
        raw = sb("raw", [P, 3, KT * GW])
        w_hi = sb("w_hi", [P, KT * 6 * GW], F32R)
        w_lo = sb("w_lo", [P, KT * 6 * GW], F32R)
        wo_hi = sb("wo_hi", [P, HEADS, DM], F32R)
        wo_lo = sb("wo_lo", [P, HEADS, DM], F32R)
        raw1 = sb("raw1", [P, KT, HIDDEN])
        raw3 = sb("raw3", [P, KT, HIDDEN])
        raw2 = sb("raw2", [P, HC, DM])
        xc_hi = sb("xc_hi", [P, KT, P], F32R)
        xc_lo = sb("xc_lo", [P, KT, P], F32R)
        rc = [sb(f"rope_cos{i}", [P, GW]) for i in range(2)]
        rs = [sb(f"rope_sin{i}", [P, GW]) for i in range(2)]
        q_rot = [sb(f"q_rot{g}", [P, GW]) for g in range(GROUPS)]
        k_rot = sb("k_rot", [P, GW])
        q_exp = sb("q_exp", [P, GW])
        q_relu = sb("q_relu", [P, GW])
        k_exp = sb("k_exp", [P, GW])
        k_relu = sb("k_relu", [P, GW])
        qf = [sb(f"qf{i}", [P, GW]) for i in range(2)]
        kf = [sb(f"kf{i}", [P, GW]) for i in range(2)]
        kf_t = [sb(f"kf_t{i}", [P, GW]) for i in range(2)]
        v1 = [sb(f"v1_{i}", [P, GROUPS, VS]) for i in range(2)]
        state = sb("state", [P, GROUPS, VS])
        probs = sb("probs", [P, GW])
        den = sb("den", [P, REP])
        rden = sb("rden", [P, REP])
        attn = sb("attn", [P, GW])
        at_hi = sb("at_hi", [P, GW], F32R)
        at_lo = sb("at_lo", [P, GW], F32R)
        res = sb("res", [P, DM])
        stats = sb("stats", [P, 6])
        mv = sb("mv", [P, 2])
        veps = sb("veps", [P, 1])
        rstd = sb("rstd", [P, 1])
        neg_half = sb("neg_half", [P, TILES])
        x1c = sb("x1c", [P, DM])
        x1t_hi = sb("x1t_hi", [P, KT, S], F32R)
        x1t_lo = sb("x1t_lo", [P, KT, S], F32R)
        ones = sb("ones", [P, P])
        wsum = sb("wsum", [P, 4])
        scale = sb("scale", [P, 12])
        T1 = w_hi[:, 0:KT * HIDDEN].rearrange("p (k n) -> p k n", k=KT)
        T3 = w_hi[:, KT * HIDDEN:2 * KT * HIDDEN].rearrange("p (k n) -> p k n", k=KT)
        T2 = w_hi[:, 2 * KT * HIDDEN:2 * KT * HIDDEN + HC * DM].rearrange("p (j n) -> p j n", j=HC)
        g_hi = w_lo[:, 0:HC * HALF_S].rearrange("p (j n) -> p j n", j=HC)
        g_lo = w_lo[:, HC * HALF_S:2 * HC * HALF_S].rearrange("p (j n) -> p j n", j=HC)
        w_hi_u = w_hi[:, :].rearrange("p (u k n) -> p u k n", u=6, k=KT)
        w_lo_u = w_lo[:, :].rearrange("p (u k n) -> p u k n", u=6, k=KT)
        below = [q_rot[0], q_rot[1], q_rot[2]]
        tanh_h = [rc[0], rc[1]]
        gate_a = rs[0]
        gate = [qf[0], qf[1]]
        r2 = [kf[0], kf[1]]

        ps = ctx.enter_context(nc.psum_tensor("ps", [P, 8, 512], F32))
        proj_ps = [ps[:, 0, :], ps[:, 1, :]]
        turn_ps = ps[:, 2, :]
        score_ps = ps[:, 3, :]
        o_ps = ps[:, 4:6, 0:2 * VS].rearrange("p b (h w) -> p b h w", w=VS)
        upd_ps = ps[:, 4, 2 * VS:2 * VS + VW]
        at_ps = ps[:, 6, :]
        y_ps = ps[:, 7, 0:DM]
        h1_ps = [ps[:, 0, :], ps[:, 1, :]]
        h3_ps = [ps[:, 2, :], ps[:, 3, :]]
        y2_ps = [ps[:, 4 + s, 0:DM] for s in range(TILES)]

        s_const = sem("tables_loaded")
        s_xt = sem("xt_loaded")
        s_x = sem("x_loaded")
        s_w = [sem(f"weight_slot_loaded{i}") for i in range(3)]
        s_ffn = sem("ffn_weights_loaded")
        s_set = sem("buffers_set")
        s_whi = sem("weight_high_split")
        s_wlo = sem("weight_low_split")
        p_k = stage("k_projected")
        p_v = stage("v_projected")
        p_q = stage("q_projected", GROUPS)
        p_qt = stage("q_turned", GROUPS)
        p_kt = stage("k_turned")
        p_sc = stage("scores_ready", GROUPS)
        p_o = stage("attended", GROUPS)
        p_at = stage("attn_turned", GROUPS)
        p_y = stage("y_ready")
        p_x1t = stage("x1_turned")
        p_sum = sem("weight_sums_ready")
        a_x = stage("x_high_split")
        a_q = stage("q_exp_relu", GROUPS)
        a_k = stage("k_exp_relu")
        a_kt = stage("kt_copied")
        a_v = stage("v_copied")
        a_at = stage("attn_high_split", GROUPS)
        a_x1 = stage("x1_high_split")
        a_abs = sem("weights_summed")
        v_x = stage("x_low_split")
        v_kr = stage("k_multiplied")
        v_qr = stage("q_multiplied", GROUPS)
        v_kf = stage("kf_ready")
        v_qf = stage("qf_ready", GROUPS)
        v_pr = stage("probs_ready", GROUPS)
        v_den = sem("den_ready")
        v_rden = stage("rden_ready", GROUPS)
        v_de = stage("den_eps_ready", GROUPS)
        v_at = stage("attn_ready", GROUPS)
        v_st = stage("state_ready", GROUPS)
        v_al = stage("attn_low_split", GROUPS)
        v_y = stage("residual_added")
        v_bs = stage("stats_ready")
        v_mv = stage("mean_ready")
        v_ve = stage("variance_ready")
        v_x1 = stage("x1_ready")
        v_xl = stage("x1_low_split")
        v_scale = sem("weight_scales_ready")
        v_neg = sem("below_ready")
        v_t = sem("ternary_ready")
        g_k = stage("k_rotated")
        g_q = stage("q_rotated", GROUPS)
        g_rs = stage("rstd_ready")
        g_x1 = stage("x1_kept")
        f_h1 = stage("h1_ready", HC, FFN_LOOP)
        f_h3 = stage("h3_ready", HC, FFN_LOOP)
        f_y = stage("y2_ready", 1, FFN_LOOP)
        f_yj = stage("y2_added", HC, FFN_LOOP)
        f_th = stage("tanh_ready", HC, FFN_LOOP)
        f_gh = stage("gate_high_split", HC, FFN_LOOP)
        f_a = stage("gate_silu_ready", HC, FFN_LOOP)
        f_g = stage("gate_ready", HC, FFN_LOOP)
        f_gl = stage("gate_low_split", HC, FFN_LOOP)
        f_r = stage("y2_residual_added", TILES, FFN_LOOP)
        f_bs = stage("y2_stats_ready", TILES, FFN_LOOP)
        f_mv = stage("y2_mean_ready", TILES, FFN_LOOP)
        f_ve = stage("y2_variance_ready", 1, FFN_LOOP)
        f_rs = stage("y2_rstd_ready", 1, FFN_LOOP)
        f_o = stage("out_ready", TILES, FFN_LOOP)
        s_out = sem("out_stored")

        def start_at_one_round(eng, *stages):
            for st in stages:
                eng.sem_inc(st.sem, st.whole)

        def ends(inst, st):
            inst.then_inc(st.sem, st.step)

        mv2 = sb("mv2", [P, TILES, 2])
        stats2 = sb("stats2", [P, TILES, 6])
        veps2 = sb("veps2", [P, TILES])
        rstd2 = sb("rstd2", [P, TILES])

        UNITS = ["k", 0, "v", 1, 2, 3]
        wd = {"k": wk_t, "v": wv_t}
        srcs = []
        for u in UNITS:
            src = wd[u] if u in wd else wq_t[:, u * GW:(u + 1) * GW]
            srcs.append(src.rearrange("(k p) n -> p k n", p=P))
        for g in range(GROUPS):
            srcs.append(wo_t[g * GW:(g + 1) * GW, :].rearrange("(h p) n -> p h n", p=P))
        NW = len(srcs)

        def raw_piece(i):
            return raw[:, i % 3, :].rearrange("p (k n) -> p k n", k=srcs[i].shape[1])

        def split_piece(i):
            if i < 6:
                return w_hi_u[:, i], w_lo_u[:, i]
            g = i - 6
            return wo_hi[:, REP * g:REP * (g + 1), :], wo_lo[:, REP * g:REP * (g + 1), :]

        def unit_weights(u):
            i = UNITS.index(u)
            return w_hi_u[:, i], w_lo_u[:, i]

        def bank(u):
            return proj_ps[UNITS.index(u) % 2]

        block = ctx.enter_context(nc.Block())

        @block.sync
        def _(sp):
            sp.dma_start(xt_all[:, :, :], x_t.rearrange("(k p) s -> p k s", p=P)).then_inc(s_xt, 16)
            for i in range(NW):
                if i >= 3:
                    sp.wait_ge(s_wlo, i - 2)
                sp.dma_start(raw_piece(i), srcs[i]).then_inc(s_w[i % 3], 16)
                if i == 0:
                    sp.dma_start(const[:, :], tables).then_inc(s_const, 16)
            sp.dma_start(x_all[:, :, :], x_seq.rearrange("(c p) d -> p c d", p=P)).then_inc(s_x, 16)
            sp.dma_start(raw1[:, :, :], w1_t.rearrange("(k p) n -> p k n", p=P)).then_inc(s_ffn, 16)
            sp.dma_start(raw3[:, :, :], w3_t.rearrange("(k p) n -> p k n", p=P)).then_inc(s_ffn, 16)
            full = (HC - 1) * HW
            sp.dma_start(raw2[0:HW, 0:HC - 1, :],
                         w2_t[0:full, :].rearrange("(j p) n -> p j n", p=HW)).then_inc(s_ffn, 16)
            sp.dma_start(raw2[0:HID[-1], HC - 1, :], w2_t[full:HIDDEN, :]).then_inc(s_ffn, 16)
            with sp.Fori(0, (HALVES - 1) * FFN_LOOP + 1, FFN_LOOP) as half:
                for s in range(TILES):
                    sp.wait_ge(f_o.sem, f_o.done(half, s))
                    row = half // FFN_LOOP * TILES + s
                    sp.dma_start(out.rearrange("(c p) d -> p c d", p=P)[:, bass.ds(row, 1), :],
                                 x_all[:, bass.ds(row, 1), :]).then_inc(s_out, 16)
            sp.wait_ge(s_out, 16 * CHUNKS)

        @block.tensor
        def _(pe):
            start_at_one_round(pe, p_k, p_v, p_q, p_qt, p_kt, p_sc, p_o, p_at, p_y, p_x1t,
                               f_h1, f_h3, f_y, f_yj)

            def project(c, u):
                hi, lo = unit_weights(u)
                if u == "k":
                    pe.wait_ge(a_x.sem, a_x.done(c))
                    pe.wait_ge(v_x.sem, v_x.done(c))
                    pe.wait_ge(v_qr.sem, v_qr.done(c - LOOP, 2))
                elif u == 0:
                    pe.wait_ge(v_qr.sem, v_qr.done(c, -1))
                elif u == "v":
                    pe.wait_ge(v_kr.sem, v_kr.done(c))
                elif u == 1:
                    pe.wait_ge(v_qr.sem, v_qr.done(c, 0))
                elif u == 2:
                    pe.wait_ge(a_v.sem, a_v.done(c))
                else:
                    pe.wait_ge(v_qr.sem, v_qr.done(c, 1))
                parts = [(xc_lo, hi), (xc_hi, lo), (xc_hi, hi)]
                for k in range(KT):
                    for n, (xp, wp) in enumerate(parts):
                        last = nc.tensor.matmul(bank(u), xp[:, k, :], wp[:, k, :],
                                                start=(k == 0 and n == 0), stop=(k == KT - 1 and n == 2))
                ends(last, {"k": p_k, "v": p_v}.get(u, p_q))

            def turn_q(c, g, k_between=False):
                pe.wait_ge(g_q.sem, g_q.done(c, g))
                if g == 0:
                    pe.wait_ge(a_kt.sem, a_kt.done(c))
                else:
                    pe.wait_ge(a_q.sem, a_q.done(c, g - 1))
                for h in range(REP):
                    last = nc.tensor.transpose(turn_ps[:, h * P:(h + 1) * P],
                                               q_rot[g][:, h * HD:(h + 1) * HD], ident)
                ends(last, p_qt)

            def turn_k(c, par):
                pe.wait_ge(v_kf.sem, v_kf.done(c))
                pe.wait_ge(a_q.sem, a_q.done(c, -1))
                for g in range(GROUPS):
                    last = nc.tensor.transpose(turn_ps[:, g * P:(g + 1) * P],
                                               kf[par][:, g * HD:(g + 1) * HD], ident)
                ends(last, p_kt)

            def scores(c, g, par):
                pe.wait_ge(v_qf.sem, v_qf.done(c, g))
                pe.wait_ge(a_kt.sem, a_kt.done(c))
                pe.wait_ge(v_pr.sem, v_pr.done(c, g - 1))
                last = nc.tensor.matmul(score_ps, kf_t[par][:, g * P:(g + 1) * P], qf[g % 2][:, :],
                                        start=True, stop=True)
                ends(last, p_sc)

            def attend(c, g, par):
                pe.wait_ge(v_pr.sem, v_pr.done(c, g))
                pe.wait_ge(a_v.sem, a_v.done(c))
                pe.wait_ge(v_st.sem, v_st.done(c, g - 1))
                pe.wait_ge(v_at.sem, v_at.done(c, g - 1))
                for h in range(REP):
                    o = o_ps[:, h // 2, h % 2, 0:VW]
                    nc.tensor.matmul(o, probs[:, h * P:(h + 1) * P], v1[par][:, g, 0:VW],
                                     start=True, stop=False)
                    nc.tensor.matmul(o, qf[g % 2][:, h * P:(h + 1) * P], state[:, g, 0:VW],
                                     start=False, stop=True)
                last = nc.tensor.matmul(upd_ps, kf[par][:, g * HD:(g + 1) * HD], v1[par][:, g, 0:VW],
                                        start=True, stop=True)
                ends(last, p_o)

            def turn_attn(c, g):
                pe.wait_ge(v_at.sem, v_at.done(c, g))
                pe.wait_ge(v_al.sem, v_al.done(c, g - 1))
                if g == 1:
                    pe.wait_ge(v_xl.sem, v_xl.done(c - LOOP))
                for h in range(REP):
                    last = nc.tensor.transpose(at_ps[:, h * P:(h + 1) * P],
                                               attn[:, h * HD:(h + 1) * HD], ident)
                ends(last, p_at)

            def out_project(c, g):
                pe.wait_ge(v_al.sem, v_al.done(c, g))
                if g == 0:
                    pe.wait_ge(v_y.sem, v_y.done(c, -1))
                for h in range(REP):
                    hh = g * REP + h
                    parts = [(at_lo, wo_hi), (at_hi, wo_lo), (at_hi, wo_hi)]
                    for n, (ap, wp) in enumerate(parts):
                        last = nc.tensor.matmul(y_ps, ap[:, h * P:(h + 1) * P], wp[:, hh, :],
                                                start=(hh == 0 and n == 0),
                                                stop=(hh == HEADS - 1 and n == 2))
                if g == GROUPS - 1:
                    ends(last, p_y)

            def turn_x1(c):
                pe.wait_ge(v_x1.sem, v_x1.done(c))
                pe.wait_ge(v_al.sem, v_al.done(c + LOOP, 0))
                for k in range(KT):
                    last = nc.tensor.transpose(at_ps[:, k * P:(k + 1) * P],
                                               x1c[:, k * P:(k + 1) * P], ident)
                ends(last, p_x1t)

            def slot(c, g, par, more=True, first=False, x1=True):
                if g < GROUPS - 1:
                    turn_q(c, g + 1)
                elif more:
                    turn_q(c + LOOP, 0)
                scores(c, g, par)
                if not first:
                    turn_attn(c if g else c - LOOP, (g - 1) % GROUPS)
                if more:
                    for u in [["k", 0], ["v", 1], [2], [3]][g]:
                        project(c + LOOP, u)
                attend(c, g, par)
                if not first:
                    out_project(c if g else c - LOOP, (g - 1) % GROUPS)
                if g == 1 and x1:
                    turn_x1(c - LOOP)
                if g == 2 and more:
                    turn_k(c + LOOP, 1 - par)

            pe.wait_ge(s_set, 1)
            for i, u in enumerate(UNITS):
                pe.wait_ge(s_wlo, i + 1)
                project(0, u)
            pe.wait_ge(s_const, 16)
            turn_k(0, 0)
            turn_q(0, 0)
            slot(0, 0, 0, first=True)
            pe.wait_ge(s_wlo, NW)
            slot(0, 1, 0, x1=False)
            with pe.Fori(0, (CHUNKS // 2 - 2) * 2 * LOOP + 1, 2 * LOOP) as c:
                slot(c, 2, 0)
                slot(c, 3, 0)
                for g in range(GROUPS):
                    slot(c + LOOP, g, 1)
                slot(c + 2 * LOOP, 0, 0)
                slot(c + 2 * LOOP, 1, 0)
            c6, c7 = (CHUNKS - 2) * LOOP, (CHUNKS - 1) * LOOP
            slot(c6, 2, 0)
            slot(c6, 3, 0)
            for g in range(GROUPS):
                slot(c7, g, 1, more=False)
            turn_attn(c7, GROUPS - 1)
            out_project(c7, GROUPS - 1)
            pe.wait_ge(a_abs, 4)
            pe.wait_ge(v_pr.sem, v_pr.done(c7, GROUPS - 1))
            nc.tensor.matmul(score_ps[:, 0:4], ones[:, :], wsum[:, :], start=True, stop=True).then_inc(p_sum, 1)
            pe.wait_ge(v_x1.sem, v_x1.done(c7))
            pe.wait_ge(v_al.sem, v_al.done(c7, GROUPS - 1))
            for k in range(KT):
                last = nc.tensor.transpose(at_ps[:, k * P:(k + 1) * P], x1c[:, k * P:(k + 1) * P], ident)
            ends(last, p_x1t)

            pe.wait_ge(v_t, 3)
            pe.wait_ge(v_xl.sem, v_xl.done(c7))
            with pe.Fori(0, (HALVES - 1) * FFN_LOOP + 1, FFN_LOOP) as half:
                cols = half // FFN_LOOP * HALF_S

                def hidden(T, dst, j):
                    for k in range(KT):
                        for n, xp in enumerate([x1t_lo, x1t_hi]):
                            last = nc.tensor.matmul(dst[0:HID[j], :], T[:, k, j * HW:j * HW + HID[j]],
                                                    xp[:, k, bass.ds(cols, HALF_S)],
                                                    start=(k == 0 and n == 0), stop=(k == KT - 1 and n == 1))
                    return last

                def down(j):
                    pe.wait_ge(f_gl.sem, f_gl.done(half, j))
                    if j == 0:
                        pe.wait_ge(f_r.sem, f_r.done(half, -1))
                    for s in range(TILES):
                        for n, gp in enumerate([g_lo, g_hi]):
                            last = nc.tensor.matmul(y2_ps[s], gp[0:HID[j], j, s * P:(s + 1) * P],
                                                    T2[0:HID[j], j, :], start=(j == 0 and n == 0),
                                                    stop=(j == HC - 1 and n == 1))
                    ends(last, f_yj)

                for j in range(HC):
                    pe.wait_ge(f_g.sem, f_g.done(half, j - 2))
                    ends(hidden(T1, h1_ps[j % 2], j), f_h1)
                    ends(hidden(T3, h3_ps[j % 2], j), f_h3)
                    if j >= 2:
                        down(j - 2)
                down(HC - 2)
                down(HC - 1)

        @block.scalar
        def _(act):
            start_at_one_round(act, a_x, a_q, a_k, a_kt, a_v, a_at, a_x1, f_th, f_gh)

            def copy(out_ap, in_ap):
                return nc.scalar.activation(out_ap, in_ap, ACT.Copy)

            def split_x(c):
                act.wait_ge(p_q.sem, p_q.done(c, -1))
                ends(copy(xc_hi[:, :, :], xt_all[:, :, bass.ds(c * (P // LOOP), P)]), a_x)

            def split_weight(i):
                act.wait_ge(s_w[i % 3], 16 * (i // 3 + 1))
                copy(split_piece(i)[0], raw_piece(i)).then_inc(s_whi, 1)

            def q_parts(c, g):
                act.wait_ge(p_qt.sem, p_qt.done(c, g))
                act.wait_ge(v_qf.sem, v_qf.done(c, g - 1))
                nc.scalar.activation(q_exp[:, :], turn_ps, ACT.Exp)
                ends(nc.scalar.activation(q_relu[:, :], turn_ps, ACT.Relu), a_q)

            def k_parts(c):
                act.wait_ge(g_k.sem, g_k.done(c))
                act.wait_ge(v_kf.sem, v_kf.done(c, -1))
                nc.scalar.activation(k_exp[:, :], k_rot[:, :], ACT.Exp)
                ends(nc.scalar.activation(k_relu[:, :], k_rot[:, :], ACT.Relu), a_k)

            def copy_v(c, par):
                act.wait_ge(p_v.sem, p_v.done(c))
                act.wait_ge(p_o.sem, p_o.done(c - 2 * LOOP, GROUPS - 1))
                ends(copy(v1[par][:, :, 0:HD], bank("v").rearrange("p (g d) -> p g d", g=GROUPS)), a_v)

            def copy_kt(c, par):
                act.wait_ge(p_kt.sem, p_kt.done(c))
                act.wait_ge(p_o.sem, p_o.done(c - 2 * LOOP, GROUPS - 1))
                ends(copy(kf_t[par][:, :], turn_ps), a_kt)

            def split_attn(c, g):
                act.wait_ge(p_at.sem, p_at.done(c, g))
                ends(copy(at_hi[:, :], at_ps), a_at)

            def split_x1(c):
                act.wait_ge(p_x1t.sem, p_x1t.done(c))
                ends(copy(x1t_hi[:, :, bass.ds(c * (P // LOOP), P)],
                          at_ps[:, 0:DM].rearrange("p (k s) -> p k s", k=KT)), a_x1)

            def slot(c, g, par, more=True, first=False, x1=True, further=True):
                if g < GROUPS - 1:
                    q_parts(c, g + 1)
                elif more:
                    q_parts(c + LOOP, 0)
                if not first:
                    split_attn(c if g else c - LOOP, (g - 1) % GROUPS)
                if g == 1 and more:
                    k_parts(c + LOOP)
                    copy_v(c + LOOP, 1 - par)
                if g == 1 and x1:
                    split_x1(c - LOOP)
                if g == 2 and more:
                    copy_kt(c + LOOP, 1 - par)
                if g == 3 and further:
                    split_x(c + 2 * LOOP)

            act.wait_ge(s_xt, 16)
            split_x(0)
            split_weight(0)
            split_weight(1)
            split_weight(2)
            k_parts(0)
            split_weight(3)
            act.wait_ge(s_set, 1)
            copy_v(0, 0)
            split_weight(4)
            split_weight(5)
            copy_kt(0, 0)
            q_parts(0, 0)
            split_x(LOOP)
            slot(0, 0, 0, first=True)
            for i in range(6, NW):
                split_weight(i)
            slot(0, 1, 0, x1=False)
            with act.Fori(0, (CHUNKS // 2 - 2) * 2 * LOOP + 1, 2 * LOOP) as c:
                slot(c, 2, 0)
                slot(c, 3, 0)
                for g in range(GROUPS):
                    slot(c + LOOP, g, 1)
                slot(c + 2 * LOOP, 0, 0)
                slot(c + 2 * LOOP, 1, 0)
            c6, c7 = (CHUNKS - 2) * LOOP, (CHUNKS - 1) * LOOP
            slot(c6, 2, 0)
            slot(c6, 3, 0, further=False)
            act.wait_ge(s_ffn, 64)
            act.wait_ge(s_set, 2)
            k2 = [k_exp, k_relu]
            trash = raw[:, :, :].rearrange("p a b -> p (a b)")
            n1 = KT * HIDDEN
            last = nc.scalar.activation(trash[:, 0:n1], raw1[:, :, :].rearrange("p k n -> p (k n)"),
                                        ACT.Abs, accum_out=wsum[:, 0:1]).then_inc(a_abs, 1)
            nc.scalar.activation(trash[:, n1:2 * n1], raw3[:, :, :].rearrange("p k n -> p (k n)"),
                                 ACT.Abs, accum_out=wsum[:, 1:2]).then_inc(a_abs, 1)
            act.wait_ge(a_abs, 2)
            n2 = (HC - 1) * DM
            nc.scalar.activation(trash[0:HW, 0:n2],
                                 raw2[0:HW, 0:HC - 1, :].rearrange("p k n -> p (k n)"),
                                 ACT.Abs, accum_out=wsum[0:HW, 2:3]).then_inc(a_abs, 1)
            nc.scalar.activation(trash[0:HID[-1], n2:n2 + DM], raw2[0:HID[-1], HC - 1, :],
                                 ACT.Abs, accum_out=wsum[0:HID[-1], 3:4]).then_inc(a_abs, 1)
            for g in range(GROUPS):
                slot(c7, g, 1, more=False, further=False)
            split_attn(c7, GROUPS - 1)
            split_x1(c7)

            act.wait_ge(v_scale, 3)
            with act.Fori(0, (HALVES - 1) * FFN_LOOP + 1, FFN_LOOP) as half:
                def split_gate(j):
                    act.wait_ge(f_g.sem, f_g.done(half, j))
                    act.wait_ge(f_yj.sem, f_yj.done(half - FFN_LOOP, j))
                    ends(copy(g_hi[0:HID[j], j, :], gate[j % 2][0:HID[j], :]), f_gh)

                for j in range(HC):
                    act.wait_ge(f_h1.sem, f_h1.done(half, j))
                    act.wait_ge(f_a.sem, f_a.done(half, j - 2))
                    ends(nc.scalar.activation(tanh_h[j % 2][0:HID[j], :], h1_ps[j % 2][0:HID[j], :],
                                              ACT.Tanh, scale=scale[0:HID[j], 6:7]), f_th)
                    if j >= 1:
                        split_gate(j - 1)
                split_gate(HC - 1)

        @block.vector
        def _(dve):
            start_at_one_round(dve, v_x, v_kr, v_qr, v_kf, v_qf, v_pr, v_rden, v_de, v_at, v_st, v_al,
                               v_y, v_bs, v_mv, v_ve, v_x1, v_xl, f_a, f_g, f_gl, f_r, f_bs, f_mv, f_ve, f_o)

            def split_x(c):
                dve.wait_ge(a_x.sem, a_x.done(c))
                ends(nc.vector.tensor_tensor(xc_lo[:, :, :], xt_all[:, :, bass.ds(c * (P // LOOP), P)],
                                             xc_hi[:, :, :].bitcast(F32), ALU.subtract), v_x)

            def split_weight(i):
                hi, lo = split_piece(i)
                dve.wait_ge(s_whi, i + 1)
                nc.vector.tensor_tensor(lo, raw_piece(i), hi.bitcast(F32), ALU.subtract).then_inc(s_wlo, 1)

            def rotate(c, u):
                n = UNITS.index(u)
                b = {"k": 0, 0: 1, 1: 0, 2: 1, 3: 0}[u]
                if u == "k":
                    dve.wait_ge(p_k.sem, p_k.done(c))
                    dve.wait_ge(g_q.sem, g_q.done(c, -1))
                else:
                    dve.wait_ge(p_q.sem, p_q.done(c, u))
                    if u == 1:
                        dve.wait_ge(g_k.sem, g_k.done(c))
                    else:
                        dve.wait_ge(g_q.sem, g_q.done(c, u - 2))
                src = bank(u).rearrange("p (a e) -> p a e", e=HALF)
                cc = cos[:, bass.ds(c * (HALF // LOOP), HALF)].unsqueeze(1).to_broadcast([P, 2 * REP, HALF])
                nc.vector.tensor_tensor(rc[b][:, :].rearrange("p (a e) -> p a e", e=HALF), src, cc, ALU.mult)
                swapped = bank(u).rearrange("p (h t e) -> p h t e", t=2, e=HALF)[:, :, ::-1, :]
                ss = sin[:, bass.ds(c * (HD // LOOP), HD)].rearrange("p (t e) -> p t e", t=2)
                ss = ss.unsqueeze(1).to_broadcast([P, REP, 2, HALF])
                last = nc.vector.tensor_tensor(rs[b][:, :].rearrange("p (h t e) -> p h t e", t=2, e=HALF),
                                               swapped, ss, ALU.mult)
                ends(last, v_kr if u == "k" else v_qr)

            def make_kf(c, par):
                dve.wait_ge(a_k.sem, a_k.done(c))
                dve.wait_ge(p_o.sem, p_o.done(c - 2 * LOOP, GROUPS - 1))
                ends(nc.vector.scalar_tensor_tensor(kf[par][:, :], k_exp[:, :], 1.0, k_relu[:, :],
                                                    ALU.min, ALU.add), v_kf)

            def make_qf(c, g):
                dve.wait_ge(a_q.sem, a_q.done(c, g))
                dve.wait_ge(p_o.sem, p_o.done(c, g - 2) if g >= 1 else p_o.done(c - LOOP, GROUPS - 2))
                ends(nc.vector.scalar_tensor_tensor(qf[g % 2][:, :], q_exp[:, :], 1.0, q_relu[:, :],
                                                    ALU.min, ALU.add), v_qf)

            def mask(c, g):
                dve.wait_ge(p_sc.sem, p_sc.done(c, g))
                dve.wait_ge(p_o.sem, p_o.done(c, g - 1))
                cb = causal.unsqueeze(1).to_broadcast([P, REP, P])
                ends(nc.vector.tensor_tensor(probs[:, :].rearrange("p (h q) -> p h q", h=REP),
                                             score_ps.rearrange("p (h q) -> p h q", h=REP), cb,
                                             ALU.mult), v_pr)

            def normalise(c, g):
                dve.wait_ge(p_o.sem, p_o.done(c, g))
                ends(nc.vector.tensor_scalar(den[:, :].rearrange("p (b h) -> p b h", b=2),
                                             o_ps[:, :, :, HD], DEN_EPS, None, ALU.add), v_de)
                ends(nc.vector.tensor_tensor(state[:, g, 0:VW], upd_ps, state[:, g, 0:VW], ALU.add), v_st)
                dve.wait_ge(v_de.sem, v_de.done(c, g))
                ends(nc.vector.reciprocal(rden[:, :], den[:, :]), v_rden)
                dve.wait_ge(v_rden.sem, v_rden.done(c, g))
                dve.wait_ge(p_at.sem, p_at.done(c, g - 1))
                rb = rden[:, :].rearrange("p (b h) -> p b h", b=2).unsqueeze(3).to_broadcast([P, 2, 2, HD])
                ends(nc.vector.tensor_tensor(attn[:, :].rearrange("p (b h d) -> p b h d", b=2, h=2),
                                             o_ps[:, :, :, 0:HD], rb, ALU.mult), v_at)

            def split_attn(c, g):
                dve.wait_ge(a_at.sem, a_at.done(c, g))
                ends(nc.vector.tensor_tensor(at_lo[:, :], at_ps, at_hi[:, :].bitcast(F32),
                                             ALU.subtract), v_al)

            def layernorm(c):
                dve.wait_ge(p_y.sem, p_y.done(c))
                ends(nc.vector.tensor_tensor(res[:, :].rearrange("p (a d) -> p a d", a=1),
                                             y_ps.rearrange("p (a d) -> p a d", a=1),
                                             x_all[:, bass.ds(c // LOOP, 1), :], ALU.add), v_y)
                dve.wait_ge(v_y.sem, v_y.done(c))
                ends(nc.vector.bn_stats(stats[:, :], res[:, :]), v_bs)
                dve.wait_ge(v_bs.sem, v_bs.done(c))
                ends(nc.vector.bn_aggr(mv[:, :], stats[:, :]), v_mv)
                dve.wait_ge(v_mv.sem, v_mv.done(c))
                ends(nc.vector.tensor_scalar(veps[:, :], mv[:, 1:2], LN_EPS, None, ALU.add), v_ve)
                dve.wait_ge(g_rs.sem, g_rs.done(c))
                dve.wait_ge(p_x1t.sem, p_x1t.done(c, -1))
                dve.wait_ge(g_x1.sem, g_x1.done(c, -1))
                ends(nc.vector.tensor_scalar(x1c[:, :], res[:, :], mv[:, 0:1], rstd[:, :],
                                             ALU.subtract, ALU.mult), v_x1)

            def split_x1(c):
                dve.wait_ge(a_x1.sem, a_x1.done(c))
                at = bass.ds(c * (P // LOOP), P)
                ends(nc.vector.tensor_tensor(x1t_lo[:, :, at],
                                             at_ps[:, 0:DM].rearrange("p (k s) -> p k s", k=KT),
                                             x1t_hi[:, :, at].bitcast(F32), ALU.subtract), v_xl)

            def slot(c, g, par, more=True, first=False, x1=True, further=True):
                mask(c, g)
                if not first:
                    split_attn(c if g else c - LOOP, (g - 1) % GROUPS)
                if g < GROUPS - 1:
                    make_qf(c, g + 1)
                elif more:
                    make_qf(c + LOOP, 0)
                if g == 1 and more:
                    make_kf(c + LOOP, 1 - par)
                if more:
                    for u in [["k", 0], [1], [2], [3]][g]:
                        rotate(c + LOOP, u)
                normalise(c, g)
                if g == 0 and not first:
                    layernorm(c - LOOP)
                if g == 1 and x1:
                    split_x1(c - LOOP)
                if g == 3 and further:
                    split_x(c + 2 * LOOP)

            for par in range(2):
                nc.vector.memset(v1[par][:, :, HD:VS], 1.0)
            nc.vector.memset(state[:, :, :], 0.0)
            nc.vector.memset(ones[:, :], 1.0)
            nc.vector.memset(neg_half[:, :], -0.5).then_inc(s_set, 1)
            nc.vector.memset(wsum[:, :], 0.0).then_inc(s_set, 1)
            dve.wait_ge(s_xt, 16)
            split_x(0)
            split_weight(0)
            split_weight(1)
            dve.wait_ge(s_const, 16)
            rotate(0, "k")
            split_weight(2)
            rotate(0, 0)
            make_kf(0, 0)
            split_weight(3)
            rotate(0, 1)
            split_weight(4)
            rotate(0, 2)
            split_weight(5)
            rotate(0, 3)
            make_qf(0, 0)
            split_x(LOOP)
            slot(0, 0, 0, first=True)
            for i in range(6, NW):
                split_weight(i)
            dve.wait_ge(s_x, 16)
            slot(0, 1, 0, x1=False)
            with dve.Fori(0, (CHUNKS // 2 - 2) * 2 * LOOP + 1, 2 * LOOP) as c:
                slot(c, 2, 0)
                slot(c, 3, 0)
                for g in range(GROUPS):
                    slot(c + LOOP, g, 1)
                slot(c + 2 * LOOP, 0, 0)
                slot(c + 2 * LOOP, 1, 0)
            c6, c7 = (CHUNKS - 2) * LOOP, (CHUNKS - 1) * LOOP
            slot(c6, 2, 0)
            slot(c6, 3, 0, further=False)
            for g in range(GROUPS):
                slot(c7, g, 1, more=False, further=False)
            split_attn(c7, GROUPS - 1)

            dve.wait_ge(p_sum, 1)
            inv = 1.0 / (HIDDEN * DM)
            nc.vector.tensor_scalar(scale[:, 0:3], score_ps[:, 0:3], inv, None, ALU.mult).then_inc(v_scale, 1)
            dve.wait_ge(v_scale, 1)
            nc.vector.scalar_tensor_tensor(scale[:, 2:3], score_ps[:, 3:4], inv, scale[:, 2:3],
                                           ALU.mult, ALU.add).then_inc(v_scale, 1)
            dve.wait_ge(v_scale, 2)
            nc.vector.tensor_scalar(scale[:, 3:6], scale[:, 0:3], 0.5, None, ALU.mult)
            nc.vector.tensor_scalar(scale[:, 8:11], scale[:, 0:3], -0.5, None, ALU.mult)
            nc.vector.tensor_scalar(scale[:, 6:7], scale[:, 0:1], 0.5, None, ALU.mult)
            nc.vector.tensor_scalar(scale[:, 7:8], scale[:, 0:1], scale[:, 1:2], 0.5, ALU.mult,
                                    ALU.mult).then_inc(v_scale, 1)
            dve.wait_ge(v_scale, 3)
            neg = raw[:, :, :].rearrange("p a b -> p (a b)")
            dve.wait_ge(a_abs, 4)
            spans = [(raw1[:, :, :].rearrange("p k n -> p (k n)"), w_hi[:, 0:n_w1], 0)
                     for n_w1 in [KT * HIDDEN]]
            spans.append((raw3[:, :, :].rearrange("p k n -> p (k n)"),
                          w_hi[:, KT * HIDDEN:2 * KT * HIDDEN], 1))
            at2 = 2 * KT * HIDDEN
            spans.append((raw2[0:HW, 0:HC - 1, :].rearrange("p k n -> p (k n)"),
                          w_hi[0:HW, at2:at2 + (HC - 1) * DM], 2))
            spans.append((raw2[0:HID[-1], HC - 1, :],
                          w_hi[0:HID[-1], at2 + (HC - 1) * DM:at2 + HC * DM], 2))
            for n, (w, t, s) in enumerate(spans):
                p, width = w.shape
                if n:
                    dve.wait_ge(v_t, n)
                nc.vector.tensor_scalar(neg[0:p, 0:width], w, scale[0:p, 8 + s:9 + s], None,
                                        ALU.is_lt).then_inc(v_neg, 1)
                dve.wait_ge(v_neg, n + 1)
                nc.vector.scalar_tensor_tensor(t, w, scale[0:p, 3 + s:4 + s], neg[0:p, 0:width],
                                               ALU.is_gt, ALU.subtract).then_inc(v_t, 1)
                if n == 0:
                    layernorm(c7)
            split_x1(c7)

            with dve.Fori(0, (HALVES - 1) * FFN_LOOP + 1, FFN_LOOP) as half:
                def gate_low(j):
                    dve.wait_ge(f_gh.sem, f_gh.done(half, j))
                    ends(nc.vector.tensor_tensor(g_lo[0:HID[j], j, :], gate[j % 2][0:HID[j], :],
                                                 g_hi[0:HID[j], j, :].bitcast(F32), ALU.subtract), f_gl)

                for j in range(HC):
                    n = HID[j]
                    dve.wait_ge(f_th.sem, f_th.done(half, j))
                    dve.wait_ge(f_g.sem, f_g.done(half, j - 1))
                    ends(nc.vector.scalar_tensor_tensor(gate_a[0:n, :], tanh_h[j % 2][0:n, :], 1.0,
                                                        h1_ps[j % 2][0:n, :], ALU.add, ALU.mult), f_a)
                    if j >= 1:
                        gate_low(j - 1)
                    dve.wait_ge(f_h3.sem, f_h3.done(half, j))
                    dve.wait_ge(f_a.sem, f_a.done(half, j))
                    ends(nc.vector.scalar_tensor_tensor(gate[j % 2][0:n, :], gate_a[0:n, :],
                                                        scale[0:n, 7:8], h3_ps[j % 2][0:n, :],
                                                        ALU.mult, ALU.mult), f_g)
                gate_low(HC - 1)

                dve.wait_ge(f_yj.sem, f_yj.done(half, HC - 1))
                for s in range(TILES):
                    row = half // FFN_LOOP * TILES + s
                    r = r2[s // 2][:, (s % 2) * DM:(s % 2 + 1) * DM]
                    ends(nc.vector.scalar_tensor_tensor(
                        r.rearrange("p (a d) -> p a d", a=1), y2_ps[s].rearrange("p (a d) -> p a d", a=1),
                        scale[:, 2:3], x_all[:, bass.ds(row, 1), :], ALU.mult, ALU.add), f_r)
                for s in range(TILES):
                    dve.wait_ge(f_r.sem, f_r.done(half, s))
                    ends(nc.vector.bn_stats(stats2[:, s, :], r2[s // 2][:, (s % 2) * DM:(s % 2 + 1) * DM]), f_bs)
                for s in range(TILES):
                    dve.wait_ge(f_bs.sem, f_bs.done(half, s))
                    ends(nc.vector.bn_aggr(mv2[:, s, :], stats2[:, s, :]), f_mv)
                dve.wait_ge(f_mv.sem, f_mv.done(half, TILES - 1))
                ends(nc.vector.tensor_scalar(veps2[:, :], mv2[:, :, 1], LN_EPS, None, ALU.add), f_ve)
                dve.wait_ge(f_rs.sem, f_rs.done(half))
                for s in range(TILES):
                    row = half // FFN_LOOP * TILES + s
                    r = r2[s // 2][:, (s % 2) * DM:(s % 2 + 1) * DM]
                    ends(nc.vector.tensor_scalar(x_all[:, bass.ds(row, 1), :],
                                                 r.rearrange("p (a d) -> p a d", a=1), mv2[:, s, 0:1], rstd2[:, s:s + 1],
                                                 ALU.subtract, ALU.mult), f_o)

        @block.gpsimd
        def _(pool):
            start_at_one_round(pool, g_k, g_q, g_rs, g_x1, f_rs)

            def add_rotation(c, u):
                b = {"k": 0, 0: 1, 1: 0, 2: 1, 3: 0}[u]
                if u == "k":
                    pool.wait_ge(v_kr.sem, v_kr.done(c))
                    pool.wait_ge(a_k.sem, a_k.done(c, -1))
                    dst, st = k_rot, g_k
                else:
                    pool.wait_ge(v_qr.sem, v_qr.done(c, u))
                    pool.wait_ge(p_qt.sem, p_qt.done(c - LOOP, u))
                    dst, st = q_rot[u], g_q
                ends(nc.gpsimd.tensor_tensor(dst[:, :], rc[b][:, :], rs[b][:, :], ALU.add), st)

            def power(c):
                pool.wait_ge(v_ve.sem, v_ve.done(c))
                ends(nc.gpsimd.tensor_tensor(rstd[:, :], veps[:, :], neg_half[:, 0:1], ALU.pow), g_rs)

            def keep_x1(c):
                pool.wait_ge(v_x1.sem, v_x1.done(c))
                ends(nc.gpsimd.tensor_copy(x_all[:, bass.ds(c // LOOP, 1), :],
                                           x1c[:, :].rearrange("p (a d) -> p a d", a=1)), g_x1)

            def slot(c, g, more=True, first=False):
                if more:
                    for u in [["k", 0], [1], [2], [3]][g]:
                        add_rotation(c + LOOP, u)
                if g == 0 and not first:
                    power(c - LOOP)
                    keep_x1(c - LOOP)

            pool.wait_ge(s_set, 1)
            for u in ["k", 0, 1, 2, 3]:
                add_rotation(0, u)
            slot(0, 0, first=True)
            slot(0, 1)
            with pool.Fori(0, (CHUNKS // 2 - 2) * 2 * LOOP + 1, 2 * LOOP) as c:
                slot(c, 2)
                slot(c, 3)
                for g in range(GROUPS):
                    slot(c + LOOP, g)
                slot(c + 2 * LOOP, 0)
                slot(c + 2 * LOOP, 1)
            c6, c7 = (CHUNKS - 2) * LOOP, (CHUNKS - 1) * LOOP
            slot(c6, 2)
            slot(c6, 3)
            slot(c7, 0, more=False)
            power(c7)
            keep_x1(c7)
            with pool.Fori(0, (HALVES - 1) * FFN_LOOP + 1, FFN_LOOP) as half:
                pool.wait_ge(f_ve.sem, f_ve.done(half))
                ends(nc.gpsimd.tensor_tensor(rstd2[:, :], veps2[:, :], neg_half[:, :], ALU.pow), f_rs)


def shape_tables():
    dim = np.arange(0, HD, 2, dtype=np.float32)
    inv_freq = (np.float32(1.0) / np.float32(ROPE_BASE) ** (dim / np.float32(HD))).astype(np.float32)
    angle = np.outer(np.arange(S, dtype=np.float32), inv_freq).astype(np.float32)
    cos, sin = np.cos(angle), np.sin(angle)
    by_chunk = lambda a: a.reshape(CHUNKS, P, -1).transpose(1, 0, 2).reshape(P, -1)
    causal = np.triu(np.ones((P, P), np.float32))
    return np.ascontiguousarray(np.concatenate(
        [causal, np.eye(P, dtype=np.float32), by_chunk(cos),
         by_chunk(np.concatenate([-sin, sin], 1))], 1).astype(np.float32))


def kernel(L0_attn_x, L0_attn_Wq, L0_attn_Wk, L0_attn_Wv, L0_attn_Wo, L0_ffn_w1, L0_ffn_w3, L0_ffn_w2):
    import concourse.bacc as bacc
    from concourse.bass_utils import run_bass_kernel_spmd

    lay = lambda a: np.ascontiguousarray(np.asarray(a))
    x = np.asarray(L0_attn_x)
    arrays = {
        "x_seq": lay(x[0]), "x_t": lay(x[0].T),
        "wq_t": lay(np.asarray(L0_attn_Wq).T), "wk_t": lay(np.asarray(L0_attn_Wk).T),
        "wv_t": lay(np.asarray(L0_attn_Wv).T), "wo_t": lay(np.asarray(L0_attn_Wo).T),
        "w1_t": lay(np.asarray(L0_ffn_w1).T), "w3_t": lay(np.asarray(L0_ffn_w3).T),
        "w2_t": lay(np.asarray(L0_ffn_w2).T), "tables": shape_tables(),
    }
    nc = bacc.Bacc("TRN2", target_bir_lowering=False, num_devices=1)
    args = [nc.dram_tensor(n, a.shape, mybir.dt.from_np(a.dtype), kind="ExternalInput").ap()
            for n, a in arrays.items()]
    out = nc.dram_tensor("out", (S, DM), F32, kind="ExternalOutput").ap()
    build(nc, *args, out)
    r = run_bass_kernel_spmd(nc, [arrays], core_ids=[0])
    return r.results[0]["out"].reshape(1, S, DM)
```

```python
from contextlib import ExitStack

import numpy as np

import concourse.bass as bass
from concourse import mybir

P = 128
F32 = mybir.dt.float32
F32R = mybir.dt.float32r
ALU = mybir.AluOpType
ACT = mybir.ActivationFunctionType

S, DM = 1024, 256
HEADS, KV_HEADS, HD = 16, 4, 128
REP = HEADS // KV_HEADS
HIDDEN = int(2 * DM * 4 / 3)
ROPE_BASE = 10000.0
DEN_EPS = 1e-6
LN_EPS = 1e-5

CHUNKS = S // P
KT = DM // P
GROUPS = KV_HEADS
GW = REP * HD
VW = HD + 1
VS = HD + 2
HALF = HD // 2

HALVES = 2
HALF_S = S // HALVES
TILES = HALF_S // P
HC = -(-HIDDEN // P)
HW = HIDDEN // HC + 1
HID = [min(HW, HIDDEN - j * HW) for j in range(HC)]
ROPE_W = HALF + HD
PIECE = KT * GW

LOOP = 4
FFN_LOOP = 12


class Stage:

    def __init__(self, sem, per, whole):
        self.sem, self.step, self.whole = sem, whole // per, whole

    def done(self, base, k=0):
        return base + self.whole + (k + 1) * self.step


def build(nc, x_seq, x_t, wq_t, wk_t, wv_t, wo_t, w1_t, w3_t, w2_t, tables, out):
    with ExitStack() as ctx:
        def sb(name, shape, dt=F32):
            return ctx.enter_context(nc.sbuf_tensor(name, shape, dt))

        def sem(name):
            return ctx.enter_context(nc.semaphore(name))

        def stage(name, per=1, whole=LOOP):
            return Stage(sem(name), per, whole)

        const = sb("const", [P, 2 * P + CHUNKS * ROPE_W])
        causal = const[:, 0:P]
        ident = const[:, P:2 * P]
        rope = const[:, 2 * P:]
        x_all = sb("x_all", [P, CHUNKS, DM])
        xt_all = sb("xt_all", [P, KT, S])
        raw = sb("raw", [P, 3 * PIECE])
        w_hi = sb("w_hi", [P, KT * 6 * GW], F32R)
        w_lo = sb("w_lo", [P, KT * 6 * GW], F32R)
        wo_hi = sb("wo_hi", [P, HEADS, DM], F32R)
        wo_lo = sb("wo_lo", [P, HEADS, DM], F32R)
        N1, N2 = KT * HIDDEN, HC * DM
        raw_ffn = sb("raw_ffn", [P, 2 * N1 + N2])
        raw1 = raw_ffn[:, 0:N1]
        raw3 = raw_ffn[:, N1:2 * N1]
        raw2 = raw_ffn[:, 2 * N1:]
        waste = raw[:, 0:N2]
        res = raw[:, N2:N2 + DM]
        x1c = raw[:, N2 + DM:N2 + 2 * DM]
        slots = [raw[:, i * PIECE:(i + 1) * PIECE] for i in range(3)]
        slots += [raw_ffn[:, i * PIECE:(i + 1) * PIECE] for i in range(4)]
        xc_hi = sb("xc_hi", [P, KT, P], F32R)
        xc_lo = sb("xc_lo", [P, KT, P], F32R)
        rc = [sb(f"rope_cos{i}", [P, GW]) for i in range(2)]
        rs = [sb(f"rope_sin{i}", [P, GW]) for i in range(2)]
        q_rot = [sb(f"q_rot{g}", [P, GW]) for g in range(GROUPS)]
        k_rot = sb("k_rot", [P, GW])
        q_exp = sb("q_exp", [P, GW])
        q_relu = sb("q_relu", [P, GW])
        k_exp, k_relu = q_exp, q_relu
        qf = [sb(f"qf{i}", [P, GW]) for i in range(2)]
        kf = [sb(f"kf{i}", [P, GW]) for i in range(2)]
        q_hi = sb("q_hi", [P, GW], F32R)
        q_lo = sb("q_lo", [P, GW], F32R)
        kt_hi = [sb(f"kt_hi{i}", [P, GW], F32R) for i in range(2)]
        kt_lo = [sb(f"kt_lo{i}", [P, GW], F32R) for i in range(2)]
        v1 = [sb(f"v1_{i}", [P, GROUPS, VS]) for i in range(2)]
        state = sb("state", [P, GROUPS, VS])
        probs = sb("probs", [P, GW])
        den = sb("den", [P, REP])
        rden = sb("rden", [P, REP])
        attn = sb("attn", [P, GW])
        at_hi = sb("at_hi", [P, GW], F32R)
        at_lo = sb("at_lo", [P, GW], F32R)
        stats = sb("stats", [P, 6])
        mv = sb("mv", [P, 2])
        veps = sb("veps", [P, 1])
        rstd = sb("rstd", [P, 1])
        neg_half = sb("neg_half", [P, TILES])
        x1t_hi = sb("x1t_hi", [P, KT, S], F32R)
        x1t_lo = sb("x1t_lo", [P, KT, S], F32R)
        mv2 = sb("mv2", [P, TILES, 2])
        stats2 = sb("stats2", [P, TILES, 6])
        veps2 = sb("veps2", [P, TILES])
        rstd2 = sb("rstd2", [P, TILES])
        shift2 = sb("shift2", [P, TILES])
        ones = sb("ones", [P, P])
        wsum = sb("wsum", [P, 4])
        scale = sb("scale", [P, 12])
        T1 = w_hi[:, 0:N1].rearrange("p (k n) -> p k n", k=KT)
        T3 = w_hi[:, N1:2 * N1].rearrange("p (k n) -> p k n", k=KT)
        T2 = w_hi[:, 2 * N1:2 * N1 + N2].rearrange("p (j n) -> p j n", j=HC)
        g_hi = w_lo[:, 0:HC * HALF_S].rearrange("p (j n) -> p j n", j=HC)
        g_lo = w_lo[:, HC * HALF_S:2 * HC * HALF_S].rearrange("p (j n) -> p j n", j=HC)
        w_hi_u = w_hi[:, :].rearrange("p (u k n) -> p u k n", u=6, k=KT)
        w_lo_u = w_lo[:, :].rearrange("p (u k n) -> p u k n", u=6, k=KT)
        tanh_h = [rc[0], rc[1]]
        gate_a = rs[0]
        gate = [rs[1], k_rot]

        ps = ctx.enter_context(nc.psum_tensor("ps", [P, 8, 512], F32))
        proj_ps = [ps[:, 0, :], ps[:, 1, :]]
        turn_ps = ps[:, 2, :]
        score_ps = ps[:, 3, :]
        o_ps = ps[:, 4:6, 0:2 * VS].rearrange("p b (h w) -> p b h w", w=VS)
        upd_ps = ps[:, 4, 2 * VS:2 * VS + VW]
        at_ps = ps[:, 6, :]
        y_ps = ps[:, 7, 0:DM]
        h_ps = [(ps[:, 0, :], ps[:, 1, :]), (ps[:, 6, :], ps[:, 7, :])]
        y2_ps = [ps[:, b, 0:DM] for b in (4, 5, 2, 3)]

        s_const = sem("first_tables_loaded")
        s_rope = sem("other_tables_loaded")
        s_xt0 = sem("first_xt_loaded")
        s_xt = sem("other_xt_loaded")
        s_x = sem("x_loaded")
        s_w = [sem(f"weight_slot_loaded{i}") for i in range(len(slots))]
        s_w1 = sem("w1_loaded")
        s_w3 = sem("w3_loaded")
        s_w2 = sem("w2_loaded")
        s_set = sem("buffers_set")
        s_whi = sem("weight_high_split")
        v_wlo = sem("weight_low_split_by_dve")
        g_wlo = sem("weight_low_split_by_pool")
        p_k = stage("k_projected")
        p_v = stage("v_projected")
        p_q = stage("q_projected", GROUPS)
        p_qt = stage("q_turned", GROUPS)
        p_kt = stage("k_turned")
        p_sc = stage("scores_ready", GROUPS)
        p_o = stage("attended", GROUPS)
        p_at = stage("attn_turned", GROUPS)
        p_y = stage("y_ready")
        p_x1t = stage("x1_turned")
        p_sum = sem("weight_sums_ready")
        a_x = stage("x_high_split")
        a_q = stage("q_exp_relu", GROUPS)
        a_qh = stage("q_high_split", GROUPS)
        a_k = stage("k_exp_relu")
        a_kt = stage("kt_high_split")
        a_v = stage("v_copied")
        a_at = stage("attn_high_split", GROUPS)
        a_x1 = stage("x1_high_split")
        a_abs = sem("w1_w2_summed")
        v_x = stage("x_low_split")
        v_kr = stage("k_multiplied")
        v_qr = stage("q_multiplied", GROUPS)
        v_kf = stage("kf_ready")
        v_kt = stage("kt_low_split")
        v_qf = stage("qf_ready", GROUPS)
        v_pr = stage("probs_ready", GROUPS)
        v_de = stage("den_eps_ready", GROUPS)
        v_rden = stage("rden_ready", GROUPS)
        v_at = stage("attn_ready", GROUPS)
        v_st = stage("state_ready", GROUPS)
        v_al = stage("attn_low_split", GROUPS)
        v_y = stage("residual_added")
        v_bs = stage("stats_ready")
        v_mv = stage("mean_ready")
        v_ve = stage("variance_ready")
        v_x1 = stage("x1_ready")
        v_xl = stage("x1_low_split")
        v_abs = sem("w3_summed")
        v_scale = sem("weight_scales_ready")
        v_neg = sem("below_ready")
        v_t = sem("ternary_ready")
        g_k = stage("k_rotated")
        g_q = stage("q_rotated", GROUPS)
        g_ql = stage("q_low_split", GROUPS)
        g_rs = stage("rstd_ready")
        g_x1 = stage("x1_kept")
        f_h = stage("h1_h3_ready", HC, FFN_LOOP)
        f_y = stage("y2_added", HC, FFN_LOOP)
        f_th = stage("tanh_ready", HC, FFN_LOOP)
        f_gh = stage("gate_high_split", HC, FFN_LOOP)
        f_a = stage("gate_silu_ready", HC, FFN_LOOP)
        f_g = stage("gate_ready", HC, FFN_LOOP)
        f_gl = stage("gate_low_split", HC, FFN_LOOP)
        f_r = stage("y2_residual_added", TILES, FFN_LOOP)
        f_bs = stage("y2_stats_ready", TILES, FFN_LOOP)
        f_mv = stage("y2_mean_ready", TILES, FFN_LOOP)
        f_ve = stage("y2_variance_ready", 1, FFN_LOOP)
        f_rs = stage("y2_rstd_ready", 1, FFN_LOOP)
        f_nb = stage("y2_shift_ready", 1, FFN_LOOP)
        f_o = stage("out_ready", TILES, FFN_LOOP)
        s_out = sem("out_stored")

        C6, C7 = (CHUNKS - 2) * LOOP, (CHUNKS - 1) * LOOP
        H0, H1 = 0, FFN_LOOP

        def start_at_one_round(eng, *stages):
            for st in stages:
                eng.sem_inc(st.sem, st.whole)

        def skip_first_chunk(eng, *stages):
            start_at_one_round(eng, *stages)

        def ends(inst, st):
            inst.then_inc(st.sem, st.step)

        def before(c, g):
            return (c, g - 1) if g else (c - LOOP, GROUPS - 1)

        UNITS = ["k", 0, "v", 1, 2, 3]
        IN_SLOT = [["k", 0], ["v", 1], [2], [3]]
        ROTATED_IN_SLOT = [["k", 0], [1], [2], [3]]
        PRODUCTS = {"k": 0, 0: 1, 1: 0, 2: 1, 3: 0}

        wd = {"k": wk_t, "v": wv_t}
        srcs = []
        for u in UNITS:
            src = wd[u] if u in wd else wq_t[:, u * GW:(u + 1) * GW]
            srcs.append(src.rearrange("(k p) n -> p k n", p=P))
        for g in range(GROUPS):
            srcs.append(wo_t[g * GW:(g + 1) * GW, :].rearrange("(h p) n -> p h n", p=P))
        NW, NU = len(srcs), len(UNITS)
        BY_POOL = [4, 8, 9]
        BY_DVE = [0, 1, 2, 3, 6, 5, 7]

        def raw_piece(i):
            return slots[i % len(slots)].rearrange("p (k n) -> p k n", k=srcs[i].shape[1])

        def split_piece(i):
            if i < NU:
                return w_hi_u[:, i], w_lo_u[:, i]
            g = i - NU
            return wo_hi[:, REP * g:REP * (g + 1), :], wo_lo[:, REP * g:REP * (g + 1), :]

        def wait_low_split(eng, i):
            if i in BY_POOL:
                eng.wait_ge(g_wlo, BY_POOL.index(i) + 1)
            else:
                eng.wait_ge(v_wlo, BY_DVE.index(i) + 1)

        def bank(u):
            return proj_ps[UNITS.index(u) % 2]

        def rows_of(c):
            return bass.ds(c * (P // LOOP), P)

        def r2(half, s):
            b = [kf[0], kf[1], probs, attn][half // FFN_LOOP * 2 + s // 2]
            return b[:, (s % 2) * DM:(s % 2 + 1) * DM]

        block = ctx.enter_context(nc.Block())

        @block.sync
        def _(sp):
            xt_src = x_t.rearrange("(k p) s -> p k s", p=P)
            early = 2 * P + ROPE_W

            def wait_used(i):
                wait_low_split(sp, i)
                if i < NU:
                    st = {"k": p_k, "v": p_v}.get(UNITS[i], p_q)
                    sp.wait_ge(st.sem, st.done(0, 0 if st is not p_q else UNITS[i]))

            def load_piece(i):
                if i >= len(slots):
                    wait_used(i - len(slots))
                sp.dma_start(raw_piece(i), srcs[i]).then_inc(s_w[i % len(slots)], 16)

            sp.dma_start(xt_all[:, :, 0:P], xt_src[:, :, 0:P]).then_inc(s_xt0, 16)
            load_piece(0)
            sp.dma_start(const[:, 0:early], tables[:, 0:early]).then_inc(s_const, 16)
            for i in range(1, NU):
                load_piece(i)
            sp.dma_start(xt_all[:, :, P:], xt_src[:, :, P:]).then_inc(s_xt, 16)
            sp.dma_start(const[:, early:], tables[:, early:]).then_inc(s_rope, 16)
            for i in range(NU, NW):
                load_piece(i)
            sp.dma_start(x_all[:, :, :], x_seq.rearrange("(c p) d -> p c d", p=P)).then_inc(s_x, 16)
            for i in range(3, len(slots)):
                wait_used(i)
            kn = "p (k n) -> p k n"
            sp.dma_start(raw1.rearrange(kn, k=KT), w1_t.rearrange("(k p) n -> p k n", p=P)).then_inc(s_w1, 16)
            sp.dma_start(raw3.rearrange(kn, k=KT), w3_t.rearrange("(k p) n -> p k n", p=P)).then_inc(s_w3, 16)
            full = (HC - 1) * HW
            sp.dma_start(raw2[0:HW, 0:(HC - 1) * DM].rearrange("p (j n) -> p j n", n=DM),
                         w2_t[0:full, :].rearrange("(j p) n -> p j n", p=HW)).then_inc(s_w2, 16)
            sp.dma_start(raw2[0:HID[-1], (HC - 1) * DM:], w2_t[full:HIDDEN, :]).then_inc(s_w2, 16)
            for half in (H0, H1):
                for s in range(TILES):
                    sp.wait_ge(f_o.sem, f_o.done(half, s))
                    row = half // FFN_LOOP * TILES + s
                    sp.dma_start(out[row * P:(row + 1) * P, :], x_all[:, row, :]).then_inc(s_out, 16)
            sp.wait_ge(s_out, 16 * CHUNKS)

        @block.tensor
        def _(pe):
            start_at_one_round(pe, p_k, p_v, p_q, p_qt, p_kt, p_sc, p_o, p_at, p_y, p_x1t, f_h, f_y)

            def project(c, u):
                if u == "k":
                    pe.wait_ge(a_x.sem, a_x.done(c))
                    pe.wait_ge(v_x.sem, v_x.done(c))
                    pe.wait_ge(v_qr.sem, v_qr.done(c - LOOP, 2))
                elif u == 0:
                    pe.wait_ge(v_qr.sem, v_qr.done(c, -1))
                elif u == "v":
                    pe.wait_ge(v_kr.sem, v_kr.done(c))
                elif u == 1:
                    pe.wait_ge(v_qr.sem, v_qr.done(c, 0))
                elif u == 2:
                    pe.wait_ge(a_v.sem, a_v.done(c))
                else:
                    pe.wait_ge(v_qr.sem, v_qr.done(c, 1))
                hi, lo = split_piece(UNITS.index(u))
                parts = [(xc_lo, hi), (xc_hi, hi), (xc_hi, lo)]
                for k in range(KT):
                    for n, (xp, wp) in enumerate(parts):
                        last = nc.tensor.matmul(bank(u), xp[:, k, :], wp[:, k, :],
                                                start=(k == 0 and n == 0), stop=(k == KT - 1 and n == 2))
                ends(last, {"k": p_k, "v": p_v}.get(u, p_q))

            def project_first(i):
                u = UNITS[i]
                pe.wait_ge(s_w[i], 16)
                if u == "v":
                    pe.wait_ge(v_kr.sem, v_kr.done(0))
                elif u == 1:
                    pe.wait_ge(v_qr.sem, v_qr.done(0, 0))
                elif u == 2:
                    pe.wait_ge(a_v.sem, a_v.done(0))
                elif u == 3:
                    pe.wait_ge(v_qr.sem, v_qr.done(0, 1))
                for k in range(KT):
                    last = nc.tensor.matmul(bank(u), xt_all[:, k, 0:P], raw_piece(i)[:, k, :],
                                            start=(k == 0), stop=(k == KT - 1))
                ends(last, {"k": p_k, "v": p_v}.get(u, p_q))

            def turn_q(c, g, first=False):
                pe.wait_ge(g_q.sem, g_q.done(c, g))
                if first:
                    pass
                elif g == 0:
                    pe.wait_ge(v_kt.sem, v_kt.done(c))
                else:
                    pe.wait_ge(a_q.sem, a_q.done(c, g - 1))
                for h in range(REP):
                    last = nc.tensor.transpose(turn_ps[:, h * P:(h + 1) * P],
                                               q_rot[g][:, h * HD:(h + 1) * HD], ident)
                ends(last, p_qt)

            def turn_k(c, par, first=False):
                pe.wait_ge(v_kf.sem, v_kf.done(c))
                pe.wait_ge(a_q.sem, a_q.done(c, 0 if first else -1))
                for g in range(GROUPS):
                    last = nc.tensor.transpose(turn_ps[:, g * P:(g + 1) * P],
                                               kf[par][:, g * HD:(g + 1) * HD], ident)
                ends(last, p_kt)

            def scores(c, g, par):
                pe.wait_ge(a_qh.sem, a_qh.done(c, g))
                pe.wait_ge(g_ql.sem, g_ql.done(c, g))
                pe.wait_ge(a_kt.sem, a_kt.done(c))
                pe.wait_ge(v_kt.sem, v_kt.done(c))
                pe.wait_ge(v_pr.sem, v_pr.done(c, g - 1))
                parts = [(kt_lo, q_hi), (kt_hi, q_hi), (kt_hi, q_lo)]
                for n, (kp, qp) in enumerate(parts):
                    last = nc.tensor.matmul(score_ps, kp[par][:, g * P:(g + 1) * P], qp[:, :],
                                            start=(n == 0), stop=(n == 2))
                ends(last, p_sc)

            def attend(c, g, par, no_state=False, last_chunk=False):
                pe.wait_ge(v_pr.sem, v_pr.done(c, g))
                pe.wait_ge(a_v.sem, a_v.done(c))
                if not last_chunk or g == 0:
                    pe.wait_ge(v_st.sem, v_st.done(c, g - 1))
                pe.wait_ge(v_at.sem, v_at.done(c, g - 1))
                for h in range(REP):
                    o = o_ps[:, h // 2, h % 2, 0:VW]
                    last = nc.tensor.matmul(o, probs[:, h * P:(h + 1) * P], v1[par][:, g, 0:VW],
                                            start=True, stop=no_state)
                    if not no_state:
                        last = nc.tensor.matmul(o, qf[g % 2][:, h * P:(h + 1) * P], state[:, g, 0:VW],
                                                start=False, stop=True)
                if not last_chunk:
                    last = nc.tensor.matmul(upd_ps, kf[par][:, g * HD:(g + 1) * HD],
                                            v1[par][:, g, 0:VW], start=True, stop=True)
                ends(last, p_o)

            def turn_attn(c, g):
                pe.wait_ge(v_at.sem, v_at.done(c, g))
                pe.wait_ge(v_al.sem, v_al.done(c, g - 1))
                if g == 1:
                    pe.wait_ge(v_xl.sem, v_xl.done(c - LOOP))
                for h in range(REP):
                    last = nc.tensor.transpose(at_ps[:, h * P:(h + 1) * P],
                                               attn[:, h * HD:(h + 1) * HD], ident)
                ends(last, p_at)

            def out_project(c, g):
                pe.wait_ge(v_al.sem, v_al.done(c, g))
                if g == 0:
                    pe.wait_ge(v_y.sem, v_y.done(c, -1))
                for h in range(REP):
                    hh = g * REP + h
                    parts = [(at_lo, wo_hi), (at_hi, wo_hi), (at_hi, wo_lo)]
                    for n, (ap, wp) in enumerate(parts):
                        last = nc.tensor.matmul(y_ps, ap[:, h * P:(h + 1) * P], wp[:, hh, :],
                                                start=(hh == 0 and n == 0),
                                                stop=(hh == HEADS - 1 and n == 2))
                if g == GROUPS - 1:
                    ends(last, p_y)

            def turn_x1(c):
                pe.wait_ge(v_x1.sem, v_x1.done(c))
                if c is C7:
                    pe.wait_ge(v_al.sem, v_al.done(c, GROUPS - 1))
                else:
                    pe.wait_ge(v_al.sem, v_al.done(c + LOOP, 0))
                for k in range(KT):
                    last = nc.tensor.transpose(at_ps[:, k * P:(k + 1) * P],
                                               x1c[:, k * P:(k + 1) * P], ident)
                ends(last, p_x1t)

            def hidden(half, j, pair):
                at = half // FFN_LOOP * HALF_S
                n = HID[j]
                for T, dst in zip((T1, T3), h_ps[pair]):
                    for k in range(KT):
                        for m, xp in enumerate([x1t_lo, x1t_hi]):
                            last = nc.tensor.matmul(dst[0:n, :], T[:, k, j * HW:j * HW + n],
                                                    xp[:, k, at:at + HALF_S],
                                                    start=(k == 0 and m == 0), stop=(k == KT - 1 and m == 1))
                ends(last, f_h)

            def down(half, j):
                pe.wait_ge(f_gl.sem, f_gl.done(half, j))
                n = HID[j]
                for s in range(TILES):
                    for m, gp in enumerate([g_lo, g_hi]):
                        last = nc.tensor.matmul(y2_ps[s], gp[0:n, j, s * P:(s + 1) * P], T2[0:n, j, :],
                                                start=(j == 0 and m == 0), stop=(j == HC - 1 and m == 1))
                ends(last, f_y)

            def slot(c, g, par, first=False, x1=True, new_w=(), new_wo=()):
                turn_q(c, g + 1) if g < GROUPS - 1 else turn_q(c + LOOP, 0)
                scores(c, g, par)
                if not first:
                    turn_attn(*before(c, g))
                for i in new_w:
                    wait_low_split(pe, i)
                for u in IN_SLOT[g]:
                    project(c + LOOP, u)
                if g == 2:
                    turn_k(c + LOOP, 1 - par)
                attend(c, g, par, no_state=not x1)
                for i in new_wo:
                    wait_low_split(pe, i)
                if not first:
                    out_project(*before(c, g))
                if g == 1 and x1:
                    turn_x1(c - LOOP)

            pe.wait_ge(s_xt0, 16)
            for i in range(NU - 2):
                project_first(i)
            pe.wait_ge(s_const, 16)
            turn_q(0, 0, first=True)
            project_first(NU - 2)
            turn_k(0, 0, first=True)
            project_first(NU - 1)
            pe.wait_ge(s_set, 1)
            pe.wait_ge(v_kt.sem, v_kt.done(0))
            slot(0, 0, 0, first=True, x1=False, new_w=(0, 1))
            slot(0, 1, 0, x1=False, new_w=(2, 3), new_wo=(NU,))
            slot(0, 2, 0, x1=False, new_w=(4,), new_wo=(NU + 1,))
            slot(0, 3, 0, x1=False, new_w=(5,), new_wo=(NU + 2,))
            wait_low_split(pe, NW - 1)
            pe.wait_ge(a_abs, 3)
            pe.wait_ge(v_abs, 1)
            pe.wait_ge(v_pr.sem, v_pr.done(0, 3))
            nc.tensor.matmul(score_ps[:, 0:4], ones[:, :], wsum[:, :], start=True, stop=True).then_inc(p_sum, 1)
            pe.wait_ge(v_scale, 2)
            with pe.Fori(LOOP, C7 - 2 * LOOP + 1, 2 * LOOP) as c:
                for g in range(GROUPS):
                    slot(c, g, 1)
                for g in range(GROUPS):
                    slot(c + LOOP, g, 0)
            for g in range(GROUPS):
                if g < GROUPS - 1:
                    turn_q(C7, g + 1)
                scores(C7, g, 1)
                turn_attn(*before(C7, g))
                if g:
                    pe.wait_ge(f_g.sem, f_g.done(H0, g - 2))
                    hidden(H0, g - 1, 0)
                attend(C7, g, 1, last_chunk=True)
                out_project(*before(C7, g))
                if g == 0:
                    pe.wait_ge(v_t, 2)
                    pe.wait_ge(v_qr.sem, v_qr.done(C7, 3))
                if g == 1:
                    turn_x1(C6)
            pe.wait_ge(f_g.sem, f_g.done(H0, 2))
            hidden(H0, 3, 0)
            turn_attn(C7, GROUPS - 1)
            pe.wait_ge(f_g.sem, f_g.done(H0, 3))
            hidden(H0, 4, 0)
            out_project(C7, GROUPS - 1)
            pe.wait_ge(f_g.sem, f_g.done(H0, 4))
            hidden(H0, 5, 0)
            pe.wait_ge(a_q.sem, a_q.done(C7, 3))
            pe.wait_ge(v_pr.sem, v_pr.done(C7, 3))
            pe.wait_ge(v_at.sem, v_at.done(C7, 3))
            pe.wait_ge(v_t, 4)
            for j in range(HC - 2):
                down(H0, j)
            turn_x1(C7)
            down(H0, HC - 2)
            down(H0, HC - 1)
            pe.wait_ge(a_x1.sem, a_x1.done(C7))
            pe.wait_ge(v_xl.sem, v_xl.done(C7))
            for j in range(HC):
                if j == 0:
                    pe.wait_ge(f_g.sem, f_g.done(H0, HC - 1))
                elif j == 1:
                    pe.wait_ge(v_y.sem, v_y.done(C7))
                else:
                    pe.wait_ge(f_g.sem, f_g.done(H1, j - 2))
                hidden(H1, j, j % 2)
                if j == 2:
                    pe.wait_ge(f_r.sem, f_r.done(H0, TILES - 1))
                if j >= 2:
                    down(H1, j - 2)
            down(H1, HC - 2)
            down(H1, HC - 1)

        @block.scalar
        def _(act):
            start_at_one_round(act, a_x, a_q, a_qh, a_k, a_kt, a_v, a_at, a_x1, f_th, f_gh, f_o)

            def copy(out_ap, in_ap):
                return nc.scalar.activation(out_ap, in_ap, ACT.Copy)

            def split_x(c):
                if c is not LOOP:
                    act.wait_ge(p_q.sem, p_q.done(c, -1))
                ends(copy(xc_hi[:, :, :], xt_all[:, :, rows_of(c)]), a_x)

            def split_weight(i):
                act.wait_ge(s_w[i % len(slots)], 16 * (i // len(slots) + 1))
                copy(split_piece(i)[0], raw_piece(i)).then_inc(s_whi, 1)

            def q_parts(c, g, k_follows=True):
                act.wait_ge(p_qt.sem, p_qt.done(c, g))
                if g == GROUPS - 1 and k_follows:
                    act.wait_ge(v_kf.sem, v_kf.done(c + LOOP))
                else:
                    act.wait_ge(v_qf.sem, v_qf.done(c, g - 1))
                nc.scalar.activation(q_exp[:, :], turn_ps, ACT.Exp)
                ends(nc.scalar.activation(q_relu[:, :], turn_ps, ACT.Relu), a_q)

            def q_high(c, g):
                act.wait_ge(v_qf.sem, v_qf.done(c, g))
                act.wait_ge(p_sc.sem, p_sc.done(c, g - 1))
                ends(copy(q_hi[:, :], qf[g % 2][:, :]), a_qh)

            def k_parts(c):
                act.wait_ge(g_k.sem, g_k.done(c))
                act.wait_ge(v_qf.sem, v_qf.done(c - LOOP, 2))
                nc.scalar.activation(k_exp[:, :], k_rot[:, :], ACT.Exp)
                ends(nc.scalar.activation(k_relu[:, :], k_rot[:, :], ACT.Relu), a_k)

            def copy_v(c, par):
                act.wait_ge(p_v.sem, p_v.done(c))
                act.wait_ge(p_o.sem, p_o.done(c - 2 * LOOP, GROUPS - 1))
                ends(copy(v1[par][:, :, 0:HD], bank("v").rearrange("p (g d) -> p g d", g=GROUPS)), a_v)

            def split_kt(c, par):
                act.wait_ge(p_kt.sem, p_kt.done(c))
                ends(copy(kt_hi[par][:, :], turn_ps), a_kt)

            def split_attn(c, g):
                act.wait_ge(p_at.sem, p_at.done(c, g))
                ends(copy(at_hi[:, :], at_ps), a_at)

            def split_x1(c):
                act.wait_ge(p_x1t.sem, p_x1t.done(c))
                ends(copy(x1t_hi[:, :, rows_of(c)],
                          at_ps[:, 0:DM].rearrange("p (k s) -> p k s", k=KT)), a_x1)

            def slot(c, g, par, first=False, x1=True, sum_weights=False):
                nxt = (c, g + 1) if g < GROUPS - 1 else (c + LOOP, 0)
                if g == 0 and not first:
                    split_x(c + LOOP)
                q_parts(*nxt)
                if not first:
                    split_attn(*before(c, g))
                if sum_weights:
                    sum_w1()
                q_high(*nxt)
                if g == 1:
                    k_parts(c + LOOP)
                    copy_v(c + LOOP, 1 - par)
                    if x1:
                        split_x1(c - LOOP)
                if g == 2:
                    split_kt(c + LOOP, 1 - par)

            def sum_w1():
                act.wait_ge(s_w1, 16)
                act.wait_ge(s_set, 2)
                for piece in (7, 8):
                    wait_low_split(act, piece)
                nc.scalar.activation(waste[:, 0:N1], raw1, ACT.Abs, accum_out=wsum[:, 0:1]).then_inc(a_abs, 1)

            def sum_w2():
                full, p, q = (HC - 1) * DM, HID[0], HID[-1]
                act.wait_ge(s_w2, 32)
                act.wait_ge(a_abs, 1)
                nc.scalar.activation(waste[0:p, 0:full], raw2[0:p, 0:full], ACT.Abs,
                                     accum_out=wsum[0:p, 2:3]).then_inc(a_abs, 1)
                act.wait_ge(a_abs, 2)
                nc.scalar.activation(waste[0:q, full:N2], raw2[0:q, full:N2], ACT.Abs,
                                     accum_out=wsum[0:q, 3:4]).then_inc(a_abs, 1)

            def tanh(half, j, pair):
                n = HID[j]
                act.wait_ge(f_h.sem, f_h.done(half, j))
                if j >= 2:
                    act.wait_ge(f_a.sem, f_a.done(half, j - 2))
                ends(nc.scalar.activation(tanh_h[j % 2][0:n, :], h_ps[pair][0][0:n, :], ACT.Tanh,
                                          scale=scale[0:n, 6:7]), f_th)

            def split_gate(half, j):
                n = HID[j]
                act.wait_ge(f_g.sem, f_g.done(half, j))
                if half == H1:
                    act.wait_ge(f_y.sem, f_y.done(H0, j))
                ends(copy(g_hi[0:n, j, :], gate[j % 2][0:n, :]), f_gh)

            def normalise(half):
                act.wait_ge(f_nb.sem, f_nb.done(half))
                for s in range(TILES):
                    row = half // FFN_LOOP * TILES + s
                    ends(nc.scalar.activation(x_all[:, row, :], r2(half, s), ACT.Identity,
                                              bias=shift2[:, s:s + 1], scale=rstd2[:, s:s + 1]), f_o)

            skip_first_chunk(act, a_x)
            for i in range(4):
                split_weight(i)
            k_parts(0)
            copy_v(0, 0)
            act.wait_ge(v_kf.sem, v_kf.done(0))
            q_parts(0, 0, k_follows=False)
            q_high(0, 0)
            split_kt(0, 0)
            act.wait_ge(s_xt, 16)
            split_x(LOOP)
            split_weight(4)
            slot(0, 0, 0, first=True, x1=False)
            for i in (5, 6):
                split_weight(i)
            slot(0, 1, 0, x1=False)
            for i in (7, 8):
                split_weight(i)
            slot(0, 2, 0, x1=False)
            split_weight(9)
            slot(0, 3, 0, x1=False, sum_weights=True)
            sum_w2()
            with act.Fori(LOOP, C7 - 2 * LOOP + 1, 2 * LOOP) as c:
                for g in range(GROUPS):
                    slot(c, g, 1)
                for g in range(GROUPS):
                    slot(c + LOOP, g, 0)
            for g in range(GROUPS):
                if g < GROUPS - 1:
                    q_parts(C7, g + 1, k_follows=False)
                split_attn(*before(C7, g))
                if g < GROUPS - 1:
                    q_high(C7, g + 1)
                if g == 1:
                    act.wait_ge(g_q.sem, g_q.done(C7, 3))
                    act.wait_ge(v_scale, 3)
                if g:
                    tanh(H0, g - 1, 0)
                if g == 1:
                    split_x1(C6)
                if g:
                    split_gate(H0, g - 1)
            tanh(H0, 3, 0)
            split_attn(C7, GROUPS - 1)
            split_gate(H0, 3)
            tanh(H0, 4, 0)
            split_gate(H0, 4)
            tanh(H0, 5, 0)
            split_gate(H0, 5)
            split_x1(C7)
            for j in range(HC):
                if j <= 1:
                    act.wait_ge(f_a.sem, f_a.done(H0, HC - 2 + j))
                tanh(H1, j, j % 2)
                if j >= 1:
                    split_gate(H1, j - 1)
                if j == 4:
                    normalise(H0)
            split_gate(H1, HC - 1)
            normalise(H1)

        @block.vector
        def _(dve):
            start_at_one_round(dve, v_x, v_kr, v_qr, v_kf, v_kt, v_qf, v_pr, v_rden, v_de, v_at, v_st,
                               v_al, v_y, v_bs, v_mv, v_ve, v_x1, v_xl, f_a, f_g, f_gl, f_r, f_bs,
                               f_mv, f_ve, f_nb)

            def split_x(c):
                dve.wait_ge(a_x.sem, a_x.done(c))
                ends(nc.vector.tensor_tensor(xc_lo[:, :, :], xt_all[:, :, rows_of(c)],
                                             xc_hi[:, :, :].bitcast(F32), ALU.subtract), v_x)

            def split_weight(i):
                hi, lo = split_piece(i)
                dve.wait_ge(s_whi, i + 1)
                nc.vector.tensor_tensor(lo, raw_piece(i), hi.bitcast(F32), ALU.subtract).then_inc(v_wlo, 1)

            def rotate(c, u):
                b = PRODUCTS[u]
                if u == "k":
                    dve.wait_ge(p_k.sem, p_k.done(c))
                    dve.wait_ge(g_q.sem, g_q.done(c, -1))
                else:
                    dve.wait_ge(p_q.sem, p_q.done(c, u))
                    if u == 1:
                        dve.wait_ge(g_k.sem, g_k.done(c))
                    else:
                        dve.wait_ge(g_q.sem, g_q.done(c, u - 2))
                cos = rope[:, bass.ds(c * (ROPE_W // LOOP), HALF)]
                sin = rope[:, bass.ds(c * (ROPE_W // LOOP) + HALF, HD)]
                src = bank(u).rearrange("p (a e) -> p a e", e=HALF)
                nc.vector.tensor_tensor(rc[b][:, :].rearrange("p (a e) -> p a e", e=HALF), src,
                                        cos.unsqueeze(1).to_broadcast([P, 2 * REP, HALF]), ALU.mult)
                halves = "p (h t e) -> p h t e"
                sin = sin.rearrange("p (t e) -> p t e", t=2).unsqueeze(1)
                last = nc.vector.tensor_tensor(rs[b][:, :].rearrange(halves, t=2, e=HALF),
                                               bank(u).rearrange(halves, t=2, e=HALF)[:, :, ::-1, :],
                                               sin.to_broadcast([P, REP, 2, HALF]), ALU.mult)
                ends(last, v_kr if u == "k" else v_qr)

            def make_kf(c, par):
                dve.wait_ge(a_k.sem, a_k.done(c))
                dve.wait_ge(p_o.sem, p_o.done(c - 2 * LOOP, GROUPS - 1))
                ends(nc.vector.scalar_tensor_tensor(kf[par][:, :], k_exp[:, :], 1.0, k_relu[:, :],
                                                    ALU.min, ALU.add), v_kf)

            def split_kt(c, par):
                dve.wait_ge(a_kt.sem, a_kt.done(c))
                ends(nc.vector.tensor_tensor(kt_lo[par][:, :], turn_ps, kt_hi[par][:, :].bitcast(F32),
                                             ALU.subtract), v_kt)

            def make_qf(c, g):
                dve.wait_ge(a_q.sem, a_q.done(c, g))
                dve.wait_ge(p_o.sem, p_o.done(c, g - 2))
                ends(nc.vector.scalar_tensor_tensor(qf[g % 2][:, :], q_exp[:, :], 1.0, q_relu[:, :],
                                                    ALU.min, ALU.add), v_qf)

            def mask(c, g):
                dve.wait_ge(p_sc.sem, p_sc.done(c, g))
                dve.wait_ge(p_o.sem, p_o.done(c, g - 1))
                hq = "p (h q) -> p h q"
                ends(nc.vector.tensor_tensor(probs[:, :].rearrange(hq, h=REP),
                                             score_ps.rearrange(hq, h=REP),
                                             causal.unsqueeze(1).to_broadcast([P, REP, P]),
                                             ALU.mult), v_pr)

            def normalise(c, g, last_chunk=False):
                dve.wait_ge(p_o.sem, p_o.done(c, g))
                ends(nc.vector.tensor_scalar(den[:, :].rearrange("p (b h) -> p b h", b=2),
                                             o_ps[:, :, :, HD], DEN_EPS, None, ALU.add), v_de)
                if not last_chunk:
                    ends(nc.vector.tensor_tensor(state[:, g, 0:VW], upd_ps, state[:, g, 0:VW],
                                                 ALU.add), v_st)
                dve.wait_ge(v_de.sem, v_de.done(c, g))
                ends(nc.vector.reciprocal(rden[:, :], den[:, :]), v_rden)
                dve.wait_ge(v_rden.sem, v_rden.done(c, g))
                dve.wait_ge(p_at.sem, p_at.done(c, g - 1))
                rb = rden[:, :].rearrange("p (b h) -> p b h", b=2).unsqueeze(3).to_broadcast([P, 2, 2, HD])
                ends(nc.vector.tensor_tensor(attn[:, :].rearrange("p (b h d) -> p b h d", b=2, h=2),
                                             o_ps[:, :, :, 0:HD], rb, ALU.mult), v_at)

            def split_attn(c, g):
                dve.wait_ge(a_at.sem, a_at.done(c, g))
                ends(nc.vector.tensor_tensor(at_lo[:, :], at_ps, at_hi[:, :].bitcast(F32),
                                             ALU.subtract), v_al)

            def residual_stats(c):
                dve.wait_ge(p_y.sem, p_y.done(c))
                ends(nc.vector.tensor_tensor(res[:, :].rearrange("p (a d) -> p a d", a=1),
                                             y_ps.rearrange("p (a d) -> p a d", a=1),
                                             x_all[:, bass.ds(c // LOOP, 1), :], ALU.add), v_y)
                dve.wait_ge(v_y.sem, v_y.done(c))
                ends(nc.vector.bn_stats(stats[:, :], res[:, :]), v_bs)
                dve.wait_ge(v_bs.sem, v_bs.done(c))
                ends(nc.vector.bn_aggr(mv[:, :], stats[:, :]), v_mv)
                dve.wait_ge(v_mv.sem, v_mv.done(c))
                ends(nc.vector.tensor_scalar(veps[:, :], mv[:, 1:2], LN_EPS, None, ALU.add), v_ve)

            def make_x1(c):
                dve.wait_ge(g_rs.sem, g_rs.done(c))
                dve.wait_ge(p_x1t.sem, p_x1t.done(c, -1))
                dve.wait_ge(g_x1.sem, g_x1.done(c, -1))
                ends(nc.vector.tensor_scalar(x1c[:, :], res[:, :], mv[:, 0:1], rstd[:, :],
                                             ALU.subtract, ALU.mult), v_x1)

            def split_x1(c):
                dve.wait_ge(a_x1.sem, a_x1.done(c))
                ends(nc.vector.tensor_tensor(x1t_lo[:, :, rows_of(c)],
                                             at_ps[:, 0:DM].rearrange("p (k s) -> p k s", k=KT),
                                             x1t_hi[:, :, rows_of(c)].bitcast(F32), ALU.subtract), v_xl)

            def sum_w3():
                dve.wait_ge(s_w3, 16)
                dve.wait_ge(s_set, 2)
                nc.vector.tensor_reduce(wsum[:, 1:2], raw3, mybir.AxisListType.X, ALU.add,
                                        apply_absolute_value=True).then_inc(v_abs, 1)

            def slot(c, g, par, first=False, x1=True, weights=(), sum_weights=False):
                if g == 0 and not first:
                    split_x(c + LOOP)
                mask(c, g)
                if not first:
                    split_attn(*before(c, g))
                if g == 1 and x1:
                    make_x1(c - LOOP)
                make_qf(c, g + 1) if g < GROUPS - 1 else make_qf(c + LOOP, 0)
                for i in weights:
                    split_weight(i)
                if sum_weights:
                    sum_w3()
                if g == 1:
                    make_kf(c + LOOP, 1 - par)
                for u in ROTATED_IN_SLOT[g]:
                    rotate(c + LOOP, u)
                if g == 2:
                    split_kt(c + LOOP, 1 - par)
                normalise(c, g)
                if g == 0 and not first:
                    residual_stats(c - LOOP)
                if g == 1 and x1:
                    split_x1(c - LOOP)

            def ternary(n, w, t, s):
                p, width = w.shape
                if n:
                    dve.wait_ge(v_t, n)
                nc.vector.tensor_scalar(waste[0:p, 0:width], w, scale[0:p, 8 + s:9 + s], None,
                                        ALU.is_lt).then_inc(v_neg, 1)
                dve.wait_ge(v_neg, n + 1)
                nc.vector.scalar_tensor_tensor(t, w, scale[0:p, 3 + s:4 + s], waste[0:p, 0:width],
                                               ALU.is_gt, ALU.subtract).then_inc(v_t, 1)

            def gate_low(half, j):
                n = HID[j]
                dve.wait_ge(f_gh.sem, f_gh.done(half, j))
                ends(nc.vector.tensor_tensor(g_lo[0:n, j, :], gate[j % 2][0:n, :],
                                             g_hi[0:n, j, :].bitcast(F32), ALU.subtract), f_gl)

            def silu_part(half, j, pair):
                n = HID[j]
                dve.wait_ge(f_th.sem, f_th.done(half, j))
                if j:
                    dve.wait_ge(f_g.sem, f_g.done(half, j - 1))
                ends(nc.vector.scalar_tensor_tensor(gate_a[0:n, :], tanh_h[j % 2][0:n, :], 1.0,
                                                    h_ps[pair][0][0:n, :], ALU.add, ALU.mult), f_a)

            def make_gate(half, j, pair):
                n = HID[j]
                dve.wait_ge(f_a.sem, f_a.done(half, j))
                ends(nc.vector.scalar_tensor_tensor(gate[j % 2][0:n, :], gate_a[0:n, :], scale[0:n, 7:8],
                                                    h_ps[pair][1][0:n, :], ALU.mult, ALU.mult), f_g)

            def residual2(half):
                dve.wait_ge(f_y.sem, f_y.done(half, HC - 1))
                for s in range(TILES):
                    row = half // FFN_LOOP * TILES + s
                    ends(nc.vector.scalar_tensor_tensor(r2(half, s), y2_ps[s], scale[:, 2:3],
                                                        x_all[:, row, :], ALU.mult, ALU.add), f_r)

            def stats_of_tiles(half):
                for s in range(TILES):
                    dve.wait_ge(f_r.sem, f_r.done(half, s))
                    ends(nc.vector.bn_stats(stats2[:, s, :], r2(half, s)), f_bs)
                for s in range(TILES):
                    dve.wait_ge(f_bs.sem, f_bs.done(half, s))
                    ends(nc.vector.bn_aggr(mv2[:, s, :], stats2[:, s, :]), f_mv)
                dve.wait_ge(f_mv.sem, f_mv.done(half, TILES - 1))
                ends(nc.vector.tensor_scalar(veps2[:, :], mv2[:, :, 1], LN_EPS, None, ALU.add), f_ve)

            def shifts(half):
                dve.wait_ge(f_rs.sem, f_rs.done(half))
                ends(nc.vector.scalar_tensor_tensor(shift2[:, :], mv2[:, :, 0], -1.0, rstd2[:, :],
                                                    ALU.mult, ALU.mult), f_nb)

            for par in range(2):
                nc.vector.memset(v1[par][:, :, HD:VS], 1.0)
            nc.vector.memset(state[:, :, :], 0.0)
            nc.vector.memset(ones[:, :], 1.0)
            nc.vector.memset(neg_half[:, :], -0.5).then_inc(s_set, 1)
            nc.vector.memset(wsum[:, :], 0.0).then_inc(s_set, 1)
            skip_first_chunk(dve, v_x)
            split_weight(0)
            dve.wait_ge(s_const, 16)
            rotate(0, "k")
            split_weight(1)
            rotate(0, 0)
            make_kf(0, 0)
            rotate(0, 1)
            split_weight(2)
            make_qf(0, 0)
            rotate(0, 2)
            split_kt(0, 0)
            rotate(0, 3)
            dve.wait_ge(s_xt, 16)
            split_x(LOOP)
            dve.wait_ge(s_rope, 16)
            split_weight(3)
            slot(0, 0, 0, first=True, x1=False)
            dve.wait_ge(s_x, 16)
            slot(0, 1, 0, x1=False, weights=(6,))
            split_weight(5)
            split_weight(7)
            slot(0, 2, 0, x1=False)
            slot(0, 3, 0, x1=False, sum_weights=True)
            inv = 1.0 / (HIDDEN * DM)
            dve.wait_ge(p_sum, 1)
            nc.vector.tensor_scalar(scale[:, 0:3], score_ps[:, 0:3], inv, None, ALU.mult).then_inc(v_scale, 1)
            dve.wait_ge(v_scale, 1)
            nc.vector.scalar_tensor_tensor(scale[:, 2:3], score_ps[:, 3:4], inv, scale[:, 2:3],
                                           ALU.mult, ALU.add).then_inc(v_scale, 1)
            dve.wait_ge(v_scale, 2)
            nc.vector.tensor_scalar(scale[:, 3:6], scale[:, 0:3], 0.5, None, ALU.mult)
            nc.vector.tensor_scalar(scale[:, 8:11], scale[:, 0:3], -0.5, None, ALU.mult)
            nc.vector.tensor_scalar(scale[:, 6:7], scale[:, 0:1], 0.5, None, ALU.mult)
            nc.vector.tensor_scalar(scale[:, 7:8], scale[:, 0:1], scale[:, 1:2], 0.5, ALU.mult,
                                    ALU.mult).then_inc(v_scale, 1)
            with dve.Fori(LOOP, C7 - 2 * LOOP + 1, 2 * LOOP) as c:
                for g in range(GROUPS):
                    slot(c, g, 1)
                for g in range(GROUPS):
                    slot(c + LOOP, g, 0)
            dve.wait_ge(v_scale, 3)
            dve.wait_ge(a_abs, 3)
            ternary(0, raw1, w_hi[:, 0:N1], 0)
            full, at2 = (HC - 1) * DM, 2 * N1
            for g in range(GROUPS):
                mask(C7, g)
                split_attn(*before(C7, g))
                if g == 1:
                    make_x1(C6)
                if g < GROUPS - 1:
                    make_qf(C7, g + 1)
                if g:
                    silu_part(H0, g - 1, 0)
                    make_gate(H0, g - 1, 0)
                if g == 0:
                    ternary(1, raw3, w_hi[:, N1:2 * N1], 1)
                normalise(C7, g, last_chunk=True)
                if g == 0:
                    residual_stats(C6)
                if g == 1:
                    split_x1(C6)
                if g:
                    gate_low(H0, g - 1)
                if g == 1:
                    ternary(2, raw2[0:HW, 0:full], w_hi[0:HW, at2:at2 + full], 2)
                    ternary(3, raw2[0:HID[-1], full:N2], w_hi[0:HID[-1], at2 + full:at2 + N2], 2)
            silu_part(H0, 3, 0)
            make_gate(H0, 3, 0)
            split_attn(C7, GROUPS - 1)
            gate_low(H0, 3)
            silu_part(H0, 4, 0)
            make_gate(H0, 4, 0)
            residual_stats(C7)
            gate_low(H0, 4)
            silu_part(H0, 5, 0)
            make_gate(H0, 5, 0)
            make_x1(C7)
            gate_low(H0, 5)
            split_x1(C7)
            for j in range(HC):
                if j == 0:
                    dve.wait_ge(f_g.sem, f_g.done(H0, HC - 1))
                silu_part(H1, j, j % 2)
                if j >= 1:
                    gate_low(H1, j - 1)
                make_gate(H1, j, j % 2)
                if j == 0:
                    dve.wait_ge(g_x1.sem, g_x1.done(C7))
                    residual2(H0)
                if j == 2:
                    stats_of_tiles(H0)
                if j == 3:
                    shifts(H0)
            gate_low(H1, HC - 1)
            residual2(H1)
            stats_of_tiles(H1)
            dve.wait_ge(f_o.sem, f_o.done(H0, TILES - 1))
            shifts(H1)

        @block.gpsimd
        def _(pool):
            start_at_one_round(pool, g_k, g_q, g_ql, g_rs, g_x1, f_rs)

            def split_weight(i):
                hi, lo = split_piece(i)
                pool.wait_ge(s_whi, i + 1)
                nc.gpsimd.tensor_tensor(lo, raw_piece(i), hi.bitcast(F32), ALU.subtract).then_inc(g_wlo, 1)

            def add_rotation(c, u):
                b = PRODUCTS[u]
                if u == "k":
                    pool.wait_ge(v_kr.sem, v_kr.done(c))
                    pool.wait_ge(a_k.sem, a_k.done(c, -1))
                    dst, st = k_rot, g_k
                else:
                    pool.wait_ge(v_qr.sem, v_qr.done(c, u))
                    pool.wait_ge(p_qt.sem, p_qt.done(c - LOOP, u))
                    dst, st = q_rot[u], g_q
                ends(nc.gpsimd.tensor_tensor(dst[:, :], rc[b][:, :], rs[b][:, :], ALU.add), st)

            def q_low(c, g):
                pool.wait_ge(a_qh.sem, a_qh.done(c, g))
                ends(nc.gpsimd.tensor_tensor(q_lo[:, :], qf[g % 2][:, :], q_hi[:, :].bitcast(F32),
                                             ALU.subtract), g_ql)

            def power(c):
                pool.wait_ge(v_ve.sem, v_ve.done(c))
                ends(nc.gpsimd.tensor_tensor(rstd[:, :], veps[:, :], neg_half[:, 0:1], ALU.pow), g_rs)

            def keep_x1(c):
                pool.wait_ge(v_x1.sem, v_x1.done(c))
                ends(nc.gpsimd.tensor_copy(x_all[:, bass.ds(c // LOOP, 1), :],
                                           x1c[:, :].rearrange("p (a d) -> p a d", a=1)), g_x1)

            def slot(c, g, first=False, x1=True):
                q_low(c, g + 1) if g < GROUPS - 1 else q_low(c + LOOP, 0)
                for u in ROTATED_IN_SLOT[g]:
                    add_rotation(c + LOOP, u)
                if g == 0 and not first:
                    power(c - LOOP)
                if g == 1 and x1:
                    keep_x1(c - LOOP)

            pool.wait_ge(s_set, 1)
            add_rotation(0, "k")
            add_rotation(0, 0)
            add_rotation(0, 1)
            q_low(0, 0)
            add_rotation(0, 2)
            add_rotation(0, 3)
            slot(0, 0, first=True)
            split_weight(4)
            slot(0, 1, x1=False)
            split_weight(8)
            slot(0, 2)
            split_weight(9)
            slot(0, 3)
            with pool.Fori(LOOP, C7 - 2 * LOOP + 1, 2 * LOOP) as c:
                for g in range(GROUPS):
                    slot(c, g)
                for g in range(GROUPS):
                    slot(c + LOOP, g)
            q_low(C7, 1)
            power(C6)
            q_low(C7, 2)
            keep_x1(C6)
            q_low(C7, 3)
            power(C7)
            keep_x1(C7)
            for half in (H0, H1):
                pool.wait_ge(f_ve.sem, f_ve.done(half))
                if half == H1:
                    pool.wait_ge(f_o.sem, f_o.done(H0, TILES - 1))
                ends(nc.gpsimd.tensor_tensor(rstd2[:, :], veps2[:, :], neg_half[:, :], ALU.pow), f_rs)


def shape_tables():
    dim = np.arange(0, HD, 2, dtype=np.float32)
    inv_freq = (np.float32(1.0) / np.float32(ROPE_BASE) ** (dim / np.float32(HD))).astype(np.float32)
    angle = np.outer(np.arange(S, dtype=np.float32), inv_freq).astype(np.float32)
    cos, sin = np.cos(angle), np.sin(angle)
    by_chunk = lambda a: a.reshape(CHUNKS, P, -1).transpose(1, 0, 2).reshape(P, -1)
    causal = np.triu(np.ones((P, P), np.float32))
    rope = by_chunk(np.concatenate([cos, -sin, sin], 1))
    return np.ascontiguousarray(np.concatenate([causal, np.eye(P, dtype=np.float32), rope], 1))


def kernel(L0_attn_x, L0_attn_Wq, L0_attn_Wk, L0_attn_Wv, L0_attn_Wo, L0_ffn_w1, L0_ffn_w3, L0_ffn_w2):
    import concourse.bacc as bacc
    from concourse.bass_utils import run_bass_kernel_spmd

    lay = lambda a: np.ascontiguousarray(np.asarray(a))
    x = np.asarray(L0_attn_x)
    arrays = {
        "x_seq": lay(x[0]), "x_t": lay(x[0].T),
        "wq_t": lay(np.asarray(L0_attn_Wq).T), "wk_t": lay(np.asarray(L0_attn_Wk).T),
        "wv_t": lay(np.asarray(L0_attn_Wv).T), "wo_t": lay(np.asarray(L0_attn_Wo).T),
        "w1_t": lay(np.asarray(L0_ffn_w1).T), "w3_t": lay(np.asarray(L0_ffn_w3).T),
        "w2_t": lay(np.asarray(L0_ffn_w2).T), "tables": shape_tables(),
    }
    nc = bacc.Bacc("TRN2", target_bir_lowering=False, num_devices=1)
    args = [nc.dram_tensor(n, a.shape, mybir.dt.from_np(a.dtype), kind="ExternalInput").ap()
            for n, a in arrays.items()]
    out = nc.dram_tensor("out", (S, DM), F32, kind="ExternalOutput").ap()
    build(nc, *args, out)
    r = run_bass_kernel_spmd(nc, [arrays], core_ids=[0])
    return r.results[0]["out"].reshape(1, S, DM)
```

```python
from contextlib import ExitStack

import numpy as np

import concourse.bass as bass
from concourse import mybir

P = 128
F32 = mybir.dt.float32
F32R = mybir.dt.float32r
ALU = mybir.AluOpType
ACT = mybir.ActivationFunctionType

S, DM = 1024, 256
HEADS, KV_HEADS, HD = 16, 4, 128
REP = HEADS // KV_HEADS
HIDDEN = int(2 * DM * 4 / 3)
ROPE_BASE = 10000.0
DEN_EPS = 1e-6
LN_EPS = 1e-5

CHUNKS = S // P
KT = DM // P
GROUPS = KV_HEADS
GW = REP * HD
VW = HD + 1
VS = HD + 2
HALF = HD // 2

HALVES = 2
HALF_S = S // HALVES
TILES = HALF_S // P
HC = -(-HIDDEN // P)
HW = HIDDEN // HC + 1
HID = [min(HW, HIDDEN - j * HW) for j in range(HC)]
ROPE_W = HALF + HD
PIECE = KT * GW

WARM_UP = 5
LOOP = 4
FFN_LOOP = 12


class Stage:

    def __init__(self, sem, per, whole):
        self.sem, self.step, self.whole = sem, whole // per, whole

    def done(self, base, k=0):
        return base + self.whole + (k + 1) * self.step

    def part_done(self, base, k, part):
        return base + self.whole + k * self.step + (part + 1) * (self.step // 2)


def build(nc, x_seq, x_t, wq_t, wk_t, wv_t, wo_t, w1_t, w3_t, w2_t, tables, out):
    with ExitStack() as ctx:
        def sb(name, shape, dt=F32):
            return ctx.enter_context(nc.sbuf_tensor(name, shape, dt))

        def sem(name):
            return ctx.enter_context(nc.semaphore(name))

        def stage(name, per=1, whole=LOOP):
            return Stage(sem(name), per, whole)

        const = sb("const", [P, 2 * P + CHUNKS * ROPE_W])
        causal = const[:, 0:P]
        ident = const[:, P:2 * P]
        rope = const[:, 2 * P:]
        x_all = sb("x_all", [P, CHUNKS, DM])
        xt_all = sb("xt_all", [P, KT, S])
        raw = sb("raw", [P, 3 * PIECE])
        w_hi = sb("w_hi", [P, KT * 6 * GW], F32R)
        w_lo = sb("w_lo", [P, KT * 6 * GW], F32R)
        wo_hi = sb("wo_hi", [P, HEADS, DM], F32R)
        wo_lo = sb("wo_lo", [P, HEADS, DM], F32R)
        N1, N2 = KT * HIDDEN, HC * DM
        raw_ffn = sb("raw_ffn", [P, 2 * N1 + N2])
        raw1 = raw_ffn[:, 0:N1]
        raw3 = raw_ffn[:, N1:2 * N1]
        raw2 = raw_ffn[:, 2 * N1:]
        res = raw[:, N2:N2 + DM]
        x1c = raw[:, N2 + DM:N2 + 2 * DM]
        slots = [raw[:, i * PIECE:(i + 1) * PIECE] for i in range(3)]
        slots += [raw_ffn[:, i * PIECE:(i + 1) * PIECE] for i in range(4)]
        xc_hi = sb("xc_hi", [P, KT, P], F32R)
        xc_lo = sb("xc_lo", [P, KT, P], F32R)
        rc = [sb(f"rope_cos{i}", [P, GW]) for i in range(2)]
        rs = [sb(f"rope_sin{i}", [P, GW]) for i in range(2)]
        q_rot = [sb(f"q_rot{g}", [P, GW]) for g in range(GROUPS)]
        k_rot = sb("k_rot", [P, GW])
        q_exp = sb("q_exp", [P, GW])
        q_relu = sb("q_relu", [P, GW])
        k_exp, k_relu = q_exp, q_relu
        qf = [sb(f"qf{i}", [P, GW]) for i in range(2)]
        kf = [sb(f"kf{i}", [P, GW]) for i in range(2)]
        q_hi = sb("q_hi", [P, GW], F32R)
        q_lo = sb("q_lo", [P, GW], F32R)
        kt_hi = [sb(f"kt_hi{i}", [P, GW], F32R) for i in range(2)]
        kt_lo = [sb(f"kt_lo{i}", [P, GW], F32R) for i in range(2)]
        v1 = [sb(f"v1_{i}", [P, GROUPS, VS]) for i in range(2)]
        state = sb("state", [P, GROUPS, VS])
        probs = sb("probs", [P, GW])
        den = sb("den", [P, REP])
        rden = sb("rden", [P, REP])
        attn = sb("attn", [P, GW])
        at_hi = sb("at_hi", [P, GW], F32R)
        at_lo = sb("at_lo", [P, GW], F32R)
        stats = sb("stats", [P, 6])
        mv = sb("mv", [P, 2])
        veps = sb("veps", [P, 1])
        rstd = sb("rstd", [P, 1])
        neg_half = sb("neg_half", [P, TILES])
        x1t_hi = sb("x1t_hi", [P, KT, S], F32R)
        x1t_lo = sb("x1t_lo", [P, KT, S], F32R)
        unread = x1t_hi[:, :, :].rearrange("p k s -> p (k s)")
        mv2 = sb("mv2", [P, CHUNKS, 2])
        stats2 = sb("stats2", [P, CHUNKS, 6])
        veps2 = sb("veps2", [P, CHUNKS])
        rstd2 = sb("rstd2", [P, CHUNKS])
        shift2 = sb("shift2", [P, CHUNKS])
        ones = sb("ones", [P, P])
        wsum = sb("wsum", [P, 4])
        scale = sb("scale", [P, 12])
        T1 = w_hi[:, 0:N1].rearrange("p (k n) -> p k n", k=KT)
        T3 = w_hi[:, N1:2 * N1].rearrange("p (k n) -> p k n", k=KT)
        T2 = w_hi[:, 2 * N1:2 * N1 + N2].rearrange("p (j n) -> p j n", j=HC)
        below1, below2 = raw[:, 0:N1], raw[:, 0:N2]
        below3 = w_hi[:, 2 * N1 + N2:3 * N1 + N2]
        g_hi = w_lo[:, 0:HC * HALF_S].rearrange("p (j n) -> p j n", j=HC)
        g_lo = w_lo[:, HC * HALF_S:2 * HC * HALF_S].rearrange("p (j n) -> p j n", j=HC)
        w_hi_u = w_hi[:, :].rearrange("p (u k n) -> p u k n", u=6, k=KT)
        w_lo_u = w_lo[:, :].rearrange("p (u k n) -> p u k n", u=6, k=KT)
        tanh_h = [rc[0], rc[1]]
        gate_a = rs[0]
        gate = [rs[1], k_rot]

        ps = ctx.enter_context(nc.psum_tensor("ps", [P, 8, 512], F32))
        proj_ps = [ps[:, 0, :], ps[:, 1, :]]
        turn_ps = ps[:, 2, :]
        score_ps = ps[:, 3, :]
        o_ps = ps[:, 4:6, 0:2 * VS].rearrange("p b (h w) -> p b h w", w=VS)
        upd_ps = ps[:, 4, 2 * VS:2 * VS + VW]
        at_ps = ps[:, 6, :]
        y_ps = ps[:, 7, 0:DM]
        sum_ps = ps[:, 0, 0:4]
        h_ps = [(ps[:, 0, :], ps[:, 1, :]), (ps[:, 2, :], ps[:, 3, :])]
        y2_ps = [ps[:, b, 0:DM] for b in (4, 5, 6, 7)]
        last_x1t_ps = ps[:, 0, 0:DM]

        s_const = sem("first_tables_loaded")
        s_rope = sem("other_tables_loaded")
        s_xt0 = sem("first_xt_loaded")
        s_xt = sem("other_xt_loaded")
        s_x = sem("x_loaded")
        s_w = [sem(f"weight_slot_loaded{i}") for i in range(len(slots))]
        s_w1 = sem("w1_loaded")
        s_w3 = sem("w3_loaded")
        s_w2 = sem("w2_loaded")
        s_ones = sem("ones_set")
        s_set = sem("buffers_set")
        s_whi = sem("weight_high_split")
        v_wlo = sem("weight_low_split_by_dve")
        g_wlo = sem("weight_low_split_by_pool")
        p_k = stage("k_projected")
        p_v = stage("v_projected")
        p_q = stage("q_projected", GROUPS)
        p_qt = stage("q_turned", GROUPS)
        p_kt = stage("k_turned")
        p_sc = stage("scores_ready", GROUPS)
        p_o = stage("attended", GROUPS)
        p_at = stage("attn_turned", GROUPS)
        p_y = stage("y_ready")
        p_x1t = stage("x1_turned")
        p_sum = sem("weight_sums_ready")
        a_x = stage("x_high_split")
        a_q = stage("q_exp_relu", GROUPS)
        a_qh = stage("q_high_split", GROUPS)
        a_k = stage("k_exp_relu")
        a_kt = stage("kt_high_split")
        a_v = stage("v_copied")
        a_at = stage("attn_high_split", GROUPS)
        a_x1 = stage("x1_high_split")
        a_abs = sem("w1_w2_summed")
        v_x = stage("x_low_split")
        v_kr = stage("k_multiplied")
        v_qr = stage("q_multiplied", GROUPS)
        v_kf = stage("kf_ready")
        v_kt = stage("kt_low_split")
        v_qf = stage("qf_ready", GROUPS)
        v_pr = stage("probs_ready", GROUPS)
        v_de = stage("den_eps_ready", GROUPS)
        v_rden = stage("rden_ready", GROUPS)
        v_at = stage("attn_ready", GROUPS)
        v_st = stage("state_ready", GROUPS)
        v_al = stage("attn_low_split", GROUPS)
        v_y = stage("residual_added")
        v_bs = stage("stats_ready")
        v_mv = stage("mean_ready")
        v_ve = stage("variance_ready")
        v_x1 = stage("x1_ready")
        v_xl = stage("x1_low_split")
        v_abs = sem("w3_summed")
        v_scale = sem("weight_scales_ready")
        g_neg = sem("below_ready")
        v_t = sem("ternary_ready")
        g_k = stage("k_rotated")
        g_q = stage("q_rotated", GROUPS)
        g_ql = stage("q_low_split", GROUPS)
        g_rs = stage("rstd_ready")
        g_x1 = stage("x1_kept")
        f_h = stage("h1_h3_ready", HC, FFN_LOOP)
        f_y = stage("y2_added", HC, FFN_LOOP)
        f_th = stage("tanh_ready", HC, FFN_LOOP)
        f_gh = stage("gate_high_split", HC, FFN_LOOP)
        f_a = stage("gate_silu_ready", HC, FFN_LOOP)
        f_g = stage("gate_ready", HC, FFN_LOOP)
        f_gl = stage("gate_low_split", HC, FFN_LOOP)
        f_r = stage("y2_residual_added", TILES, FFN_LOOP)
        f_bs = stage("y2_stats_ready", TILES, FFN_LOOP)
        f_mv = stage("y2_mean_ready", TILES, FFN_LOOP)
        f_ve = stage("y2_variance_ready", 2, FFN_LOOP)
        f_rs = stage("y2_rstd_ready", 2, FFN_LOOP)
        f_nb = stage("y2_shift_ready", 2, FFN_LOOP)
        f_o = stage("out_ready", TILES, FFN_LOOP)
        v_o = sem("last_out_ready")
        s_out = sem("out_stored")

        C6, C7 = (CHUNKS - 2) * LOOP, (CHUNKS - 1) * LOOP
        H0, H1 = 0, FFN_LOOP

        def start_at_one_round(eng, *stages):
            for st in stages:
                eng.sem_inc(st.sem, st.whole)

        def skip_first_chunk(eng, *stages):
            start_at_one_round(eng, *stages)

        def ends(inst, st, parts=1):
            inst.then_inc(st.sem, st.step // parts)

        def before(c, g):
            return (c, g - 1) if g else (c - LOOP, GROUPS - 1)

        UNITS = ["k", 0, "v", 1, 2, 3]
        IN_SLOT = [["k", 0], ["v", 1], [2], [3]]
        ROTATED_IN_SLOT = [["k", 0], [1], [2], [3]]
        PRODUCTS = {"k": 0, 0: 1, 1: 0, 2: 1, 3: 0}

        wd = {"k": wk_t, "v": wv_t}
        srcs = []
        for u in UNITS:
            src = wd[u] if u in wd else wq_t[:, u * GW:(u + 1) * GW]
            srcs.append(src.rearrange("(k p) n -> p k n", p=P))
        for g in range(GROUPS):
            srcs.append(wo_t[g * GW:(g + 1) * GW, :].rearrange("(h p) n -> p h n", p=P))
        NW, NU = len(srcs), len(UNITS)
        BY_POOL = [2, 4, 7, 8, 9]
        BY_DVE = [0, 1, 3, 6, 5]

        def raw_piece(i):
            return slots[i % len(slots)].rearrange("p (k n) -> p k n", k=srcs[i].shape[1])

        def split_piece(i):
            if i < NU:
                return w_hi_u[:, i], w_lo_u[:, i]
            g = i - NU
            return wo_hi[:, REP * g:REP * (g + 1), :], wo_lo[:, REP * g:REP * (g + 1), :]

        def wait_low_split(eng, i):
            if i in BY_POOL:
                eng.wait_ge(g_wlo, BY_POOL.index(i) + 1)
            else:
                eng.wait_ge(v_wlo, BY_DVE.index(i) + 1)

        def bank(u):
            return proj_ps[UNITS.index(u) % 2]

        def rows_of(c):
            return bass.ds(c * (P // LOOP), P)

        PARTS = [slice(0, HALF_S // 2), slice(HALF_S // 2, HALF_S)]

        def row_tile(half, s):
            return half // FFN_LOOP * TILES + s

        def r2(half, s):
            b = [kf[0], kf[1], probs, attn][half // FFN_LOOP * 2 + s // 2]
            return b[:, (s % 2) * DM:(s % 2 + 1) * DM]

        block = ctx.enter_context(nc.Block())

        @block.sync
        def _(sp):
            xt_src = x_t.rearrange("(k p) s -> p k s", p=P)
            early = 2 * P + ROPE_W

            def wait_used(i):
                wait_low_split(sp, i)
                if i < NU:
                    st = {"k": p_k, "v": p_v}.get(UNITS[i], p_q)
                    sp.wait_ge(st.sem, st.done(0, 0 if st is not p_q else UNITS[i]))

            def load_piece(i):
                if i >= len(slots):
                    wait_used(i - len(slots))
                sp.dma_start(raw_piece(i), srcs[i]).then_inc(s_w[i % len(slots)], 16)

            sp.dma_start(xt_all[:, :, 0:P], xt_src[:, :, 0:P]).then_inc(s_xt0, 16)
            load_piece(0)
            sp.dma_start(const[:, 0:early], tables[:, 0:early]).then_inc(s_const, 16)
            for i in range(1, NU):
                load_piece(i)
            sp.dma_start(xt_all[:, :, P:], xt_src[:, :, P:]).then_inc(s_xt, 16)
            sp.dma_start(const[:, early:], tables[:, early:]).then_inc(s_rope, 16)
            for i in range(NU, NW):
                load_piece(i)
            sp.dma_start(x_all[:, :, :], x_seq.rearrange("(c p) d -> p c d", p=P)).then_inc(s_x, 16)
            for i in range(3, len(slots)):
                wait_used(i)
            kn = "p (k n) -> p k n"
            sp.dma_start(raw1.rearrange(kn, k=KT), w1_t.rearrange("(k p) n -> p k n", p=P)).then_inc(s_w1, 16)
            sp.dma_start(raw3.rearrange(kn, k=KT), w3_t.rearrange("(k p) n -> p k n", p=P)).then_inc(s_w3, 16)
            full = (HC - 1) * HW
            sp.dma_start(raw2[0:HW, 0:(HC - 1) * DM].rearrange("p (j n) -> p j n", n=DM),
                         w2_t[0:full, :].rearrange("(j p) n -> p j n", p=HW)).then_inc(s_w2, 16)
            sp.dma_start(raw2[0:HID[-1], (HC - 1) * DM:], w2_t[full:HIDDEN, :]).then_inc(s_w2, 16)
            for half in (H0, H1):
                for s in range(TILES):
                    if half == H1 and s >= 2:
                        sp.wait_ge(v_o, s - 1)
                    else:
                        sp.wait_ge(f_o.sem, f_o.done(half, s))
                    row = row_tile(half, s)
                    sp.dma_start(out[row * P:(row + 1) * P, :], x_all[:, row, :]).then_inc(s_out, 16)
            sp.wait_ge(s_out, 16 * CHUNKS)

        @block.tensor
        def _(pe):
            start_at_one_round(pe, p_k, p_v, p_q, p_qt, p_kt, p_sc, p_o, p_at, p_y, p_x1t, f_h, f_y)

            def project(c, u):
                if u == "k":
                    pe.wait_ge(a_x.sem, a_x.done(c))
                    pe.wait_ge(v_x.sem, v_x.done(c))
                    pe.wait_ge(v_qr.sem, v_qr.done(c - LOOP, 2))
                elif u == 0:
                    pe.wait_ge(v_qr.sem, v_qr.done(c, -1))
                elif u == "v":
                    pe.wait_ge(v_kr.sem, v_kr.done(c))
                elif u == 1:
                    pe.wait_ge(v_qr.sem, v_qr.done(c, 0))
                elif u == 2:
                    pe.wait_ge(a_v.sem, a_v.done(c))
                else:
                    pe.wait_ge(v_qr.sem, v_qr.done(c, 1))
                hi, lo = split_piece(UNITS.index(u))
                parts = [(xc_lo, hi), (xc_hi, hi), (xc_hi, lo)]
                for k in range(KT):
                    for n, (xp, wp) in enumerate(parts):
                        last = nc.tensor.matmul(bank(u), xp[:, k, :], wp[:, k, :],
                                                start=(k == 0 and n == 0), stop=(k == KT - 1 and n == 2))
                ends(last, {"k": p_k, "v": p_v}.get(u, p_q))

            def project_first(i):
                u = UNITS[i]
                pe.wait_ge(s_w[i], 16)
                if u == "v":
                    pe.wait_ge(v_kr.sem, v_kr.done(0))
                elif u == 1:
                    pe.wait_ge(v_qr.sem, v_qr.done(0, 0))
                elif u == 2:
                    pe.wait_ge(a_v.sem, a_v.done(0))
                elif u == 3:
                    pe.wait_ge(v_qr.sem, v_qr.done(0, 1))
                for k in range(KT):
                    last = nc.tensor.matmul(bank(u), xt_all[:, k, 0:P], raw_piece(i)[:, k, :],
                                            start=(k == 0), stop=(k == KT - 1))
                ends(last, {"k": p_k, "v": p_v}.get(u, p_q))

            def turn_q(c, g, first=False):
                pe.wait_ge(g_q.sem, g_q.done(c, g))
                if first:
                    pass
                elif g == 0:
                    pe.wait_ge(v_kt.sem, v_kt.done(c))
                else:
                    pe.wait_ge(a_q.sem, a_q.done(c, g - 1))
                for h in range(REP):
                    last = nc.tensor.transpose(turn_ps[:, h * P:(h + 1) * P],
                                               q_rot[g][:, h * HD:(h + 1) * HD], ident)
                ends(last, p_qt)

            def turn_k(c, par, first=False):
                pe.wait_ge(v_kf.sem, v_kf.done(c))
                pe.wait_ge(a_q.sem, a_q.done(c, 0 if first else -1))
                for g in range(GROUPS):
                    last = nc.tensor.transpose(turn_ps[:, g * P:(g + 1) * P],
                                               kf[par][:, g * HD:(g + 1) * HD], ident)
                ends(last, p_kt)

            def scores(c, g, par):
                pe.wait_ge(a_qh.sem, a_qh.done(c, g))
                pe.wait_ge(g_ql.sem, g_ql.done(c, g))
                pe.wait_ge(a_kt.sem, a_kt.done(c))
                pe.wait_ge(v_kt.sem, v_kt.done(c))
                pe.wait_ge(v_pr.sem, v_pr.done(c, g - 1))
                parts = [(kt_lo, q_hi), (kt_hi, q_hi), (kt_hi, q_lo)]
                for n, (kp, qp) in enumerate(parts):
                    last = nc.tensor.matmul(score_ps, kp[par][:, g * P:(g + 1) * P], qp[:, :],
                                            start=(n == 0), stop=(n == 2))
                ends(last, p_sc)

            def attend(c, g, par, no_state=False, last_chunk=False):
                pe.wait_ge(v_pr.sem, v_pr.done(c, g))
                pe.wait_ge(a_v.sem, a_v.done(c))
                if not last_chunk or g == 0:
                    pe.wait_ge(v_st.sem, v_st.done(c, g - 1))
                pe.wait_ge(v_at.sem, v_at.done(c, g - 1))
                for h in range(REP):
                    o = o_ps[:, h // 2, h % 2, 0:VW]
                    last = nc.tensor.matmul(o, probs[:, h * P:(h + 1) * P], v1[par][:, g, 0:VW],
                                            start=True, stop=no_state)
                    if not no_state:
                        last = nc.tensor.matmul(o, qf[g % 2][:, h * P:(h + 1) * P], state[:, g, 0:VW],
                                                start=False, stop=True)
                if not last_chunk:
                    last = nc.tensor.matmul(upd_ps, kf[par][:, g * HD:(g + 1) * HD],
                                            v1[par][:, g, 0:VW], start=True, stop=True)
                ends(last, p_o)

            def turn_attn(c, g):
                pe.wait_ge(v_at.sem, v_at.done(c, g))
                pe.wait_ge(v_al.sem, v_al.done(c, g - 1))
                if g == (2 if c is C7 else 1):
                    pe.wait_ge(v_xl.sem, v_xl.done(c - LOOP))
                for h in range(REP):
                    last = nc.tensor.transpose(at_ps[:, h * P:(h + 1) * P],
                                               attn[:, h * HD:(h + 1) * HD], ident)
                ends(last, p_at)

            def out_project(c, g):
                pe.wait_ge(v_al.sem, v_al.done(c, g))
                if g == 0:
                    pe.wait_ge(v_y.sem, v_y.done(c, -1))
                for h in range(REP):
                    hh = g * REP + h
                    parts = [(at_lo, wo_hi), (at_hi, wo_hi), (at_hi, wo_lo)]
                    for n, (ap, wp) in enumerate(parts):
                        last = nc.tensor.matmul(y_ps, ap[:, h * P:(h + 1) * P], wp[:, hh, :],
                                                start=(hh == 0 and n == 0),
                                                stop=(hh == HEADS - 1 and n == 2))
                if g == GROUPS - 1:
                    ends(last, p_y)

            def turn_x1(c):
                pe.wait_ge(v_x1.sem, v_x1.done(c))
                if c is C7:
                    pe.wait_ge(f_g.sem, f_g.done(H0, HC - 2))
                else:
                    pe.wait_ge(v_al.sem, v_al.done(c + LOOP, 1 if c is C6 else 0))
                dst = last_x1t_ps if c is C7 else at_ps
                for k in range(KT):
                    last = nc.tensor.transpose(dst[:, k * P:(k + 1) * P],
                                               x1c[:, k * P:(k + 1) * P], ident)
                ends(last, p_x1t)

            def hidden(half, j, pair):
                at = half // FFN_LOOP * HALF_S
                n = HID[j]
                for T, dst in zip((T1, T3), h_ps[pair]):
                    for k in range(KT):
                        for m, xp in enumerate([x1t_lo, x1t_hi]):
                            last = nc.tensor.matmul(dst[0:n, :], T[:, k, j * HW:j * HW + n],
                                                    xp[:, k, at:at + HALF_S],
                                                    start=(k == 0 and m == 0), stop=(k == KT - 1 and m == 1))
                ends(last, f_h)

            def down(half, j):
                in_parts = (half, j) == (H1, HC - 1)
                if not in_parts:
                    pe.wait_ge(f_gl.sem, f_gl.done(half, j))
                n = HID[j]
                for s in range(TILES):
                    if (half, j) == (H1, 0):
                        pe.wait_ge(f_r.sem, f_r.done(H0, s))
                    if in_parts and s % 2 == 0:
                        pe.wait_ge(f_gl.sem, f_gl.part_done(half, j, s // 2))
                    for m, gp in enumerate([g_hi, g_lo]):
                        last = nc.tensor.matmul(y2_ps[s], gp[0:n, j, s * P:(s + 1) * P], T2[0:n, j, :],
                                                start=(j == 0 and m == 0), stop=(j == HC - 1 and m == 1))
                    if in_parts and s % 2:
                        ends(last, f_y, 2)
                if not in_parts:
                    ends(last, f_y)

            def slot(c, g, par, first=False, x1=True, new_w=False):
                turn_q(c, g + 1) if g < GROUPS - 1 else turn_q(c + LOOP, 0)
                scores(c, g, par)
                if not first:
                    turn_attn(*before(c, g))
                for u in IN_SLOT[g]:
                    if new_w:
                        wait_low_split(pe, UNITS.index(u))
                    project(c + LOOP, u)
                if g == 2:
                    turn_k(c + LOOP, 1 - par)
                if g == 1 and x1:
                    turn_x1(c - LOOP)
                attend(c, g, par, no_state=not x1)
                if new_w and g:
                    wait_low_split(pe, NU + g - 1)
                if not first:
                    out_project(*before(c, g))

            pe.wait_ge(s_ones, 1)
            for _ in range(WARM_UP):
                nc.tensor.matmul(ps[:, 7, 0:P], ones[:, :], ones[:, :], start=True, stop=True)
            pe.wait_ge(s_xt0, 16)
            for i in range(NU - 2):
                project_first(i)
            pe.wait_ge(s_const, 16)
            turn_q(0, 0, first=True)
            project_first(NU - 2)
            turn_k(0, 0, first=True)
            project_first(NU - 1)
            pe.wait_ge(s_set, 1)
            pe.wait_ge(v_kt.sem, v_kt.done(0))
            slot(0, 0, 0, first=True, x1=False, new_w=True)
            slot(0, 1, 0, x1=False, new_w=True)
            slot(0, 2, 0, x1=False, new_w=True)
            slot(0, 3, 0, x1=False, new_w=True)
            wait_low_split(pe, NW - 1)
            pe.wait_ge(v_qr.sem, v_qr.done(LOOP, 2))
            pe.wait_ge(a_abs, 3)
            pe.wait_ge(v_abs, 1)
            nc.tensor.matmul(sum_ps, ones[:, :], wsum[:, :], start=True, stop=True).then_inc(p_sum, 1)
            with pe.Fori(LOOP, C7 - 2 * LOOP + 1, 2 * LOOP) as c:
                for g in range(GROUPS):
                    slot(c, g, 1)
                for g in range(GROUPS):
                    slot(c + LOOP, g, 0)
            for g in range(GROUPS):
                if g < GROUPS - 1:
                    turn_q(C7, g + 1)
                scores(C7, g, 1)
                if g <= 1:
                    turn_attn(*before(C7, g))
                if g == 1:
                    pe.wait_ge(v_t, 3)
                    pe.wait_ge(v_qr.sem, v_qr.done(C7, 3))
                elif g:
                    pe.wait_ge(f_g.sem, f_g.done(H0, g - 2))
                if g == 3:
                    pe.wait_ge(v_t, 4)
                if g:
                    hidden(H0, g - 1, 0)
                if g >= 2:
                    turn_attn(*before(C7, g))
                attend(C7, g, 1, last_chunk=True)
                if g == 2:
                    turn_x1(C6)
                out_project(*before(C7, g))
            pe.wait_ge(a_q.sem, a_q.done(C7, 3))
            pe.wait_ge(v_pr.sem, v_pr.done(C7, 3))
            hidden(H0, 3, 1)
            turn_attn(C7, GROUPS - 1)
            pe.wait_ge(f_g.sem, f_g.done(H0, 2))
            hidden(H0, 4, 0)
            out_project(C7, GROUPS - 1)
            pe.wait_ge(f_g.sem, f_g.done(H0, 3))
            hidden(H0, 5, 1)
            pe.wait_ge(v_al.sem, v_al.done(C7, 3))
            pe.wait_ge(v_at.sem, v_at.done(C7, 3))
            pe.wait_ge(v_y.sem, v_y.done(C7))
            pe.wait_ge(v_t, 6)
            for j in range(HC - 1):
                down(H0, j)
                if j == 2:
                    turn_x1(C7)
            pe.wait_ge(a_x1.sem, a_x1.done(C7))
            pe.wait_ge(v_xl.sem, v_xl.done(C7))
            for j in range(HC):
                if j == 1:
                    pe.wait_ge(f_g.sem, f_g.done(H0, HC - 1))
                elif j:
                    pe.wait_ge(f_g.sem, f_g.done(H1, j - 2))
                hidden(H1, j, j % 2)
                if j == 0:
                    down(H0, HC - 1)
                if 2 <= j < HC - 2:
                    down(H1, j - 2)
            for j in range(HC - 4, HC):
                down(H1, j)

        @block.scalar
        def _(act):
            start_at_one_round(act, a_x, a_q, a_qh, a_k, a_kt, a_v, a_at, a_x1, f_th, f_gh, f_o)

            def copy(out_ap, in_ap):
                return nc.scalar.activation(out_ap, in_ap, ACT.Copy)

            def split_x(c):
                if c is not LOOP:
                    act.wait_ge(p_q.sem, p_q.done(c, -1))
                ends(copy(xc_hi[:, :, :], xt_all[:, :, rows_of(c)]), a_x)

            def split_weight(i):
                act.wait_ge(s_w[i % len(slots)], 16 * (i // len(slots) + 1))
                copy(split_piece(i)[0], raw_piece(i)).then_inc(s_whi, 1)

            def q_parts(c, g, k_follows=True):
                act.wait_ge(p_qt.sem, p_qt.done(c, g))
                if g == GROUPS - 1 and k_follows:
                    act.wait_ge(v_kf.sem, v_kf.done(c + LOOP))
                else:
                    act.wait_ge(v_qf.sem, v_qf.done(c, g - 1))
                nc.scalar.activation(q_exp[:, :], turn_ps, ACT.Exp)
                ends(nc.scalar.activation(q_relu[:, :], turn_ps, ACT.Relu), a_q)

            def q_high(c, g):
                act.wait_ge(v_qf.sem, v_qf.done(c, g))
                act.wait_ge(p_sc.sem, p_sc.done(c, g - 1))
                ends(copy(q_hi[:, :], qf[g % 2][:, :]), a_qh)

            def k_parts(c):
                act.wait_ge(g_k.sem, g_k.done(c))
                act.wait_ge(v_qf.sem, v_qf.done(c - LOOP, 2))
                nc.scalar.activation(k_exp[:, :], k_rot[:, :], ACT.Exp)
                ends(nc.scalar.activation(k_relu[:, :], k_rot[:, :], ACT.Relu), a_k)

            def copy_v(c, par):
                act.wait_ge(p_v.sem, p_v.done(c))
                act.wait_ge(p_o.sem, p_o.done(c - 2 * LOOP, GROUPS - 1))
                ends(copy(v1[par][:, :, 0:HD], bank("v").rearrange("p (g d) -> p g d", g=GROUPS)), a_v)

            def split_kt(c, par):
                act.wait_ge(p_kt.sem, p_kt.done(c))
                ends(copy(kt_hi[par][:, :], turn_ps), a_kt)

            def split_attn(c, g):
                act.wait_ge(p_at.sem, p_at.done(c, g))
                ends(copy(at_hi[:, :], at_ps), a_at)

            def split_x1(c):
                act.wait_ge(p_x1t.sem, p_x1t.done(c))
                src = last_x1t_ps if c is C7 else at_ps[:, 0:DM]
                ends(copy(x1t_hi[:, :, rows_of(c)], src.rearrange("p (k s) -> p k s", k=KT)), a_x1)

            def slot(c, g, par, first=False, x1=True, sum_weights=False):
                nxt = (c, g + 1) if g < GROUPS - 1 else (c + LOOP, 0)
                if g == 0 and not first:
                    split_x(c + LOOP)
                q_parts(*nxt)
                if not first:
                    split_attn(*before(c, g))
                if sum_weights:
                    sum_w1()
                q_high(*nxt)
                if g == 1:
                    k_parts(c + LOOP)
                    copy_v(c + LOOP, 1 - par)
                    if x1:
                        split_x1(c - LOOP)
                if g == 2:
                    split_kt(c + LOOP, 1 - par)

            def sum_w1():
                act.wait_ge(s_w1, 16)
                act.wait_ge(s_set, 2)
                nc.scalar.activation(unread[:, 0:N1], raw1, ACT.Abs, accum_out=wsum[:, 0:1]).then_inc(a_abs, 1)

            def sum_w2():
                full, p, q = (HC - 1) * DM, HID[0], HID[-1]
                act.wait_ge(s_w2, 32)
                act.wait_ge(a_abs, 1)
                nc.scalar.activation(unread[0:p, 0:full], raw2[0:p, 0:full], ACT.Abs,
                                     accum_out=wsum[0:p, 2:3]).then_inc(a_abs, 1)
                act.wait_ge(a_abs, 2)
                nc.scalar.activation(unread[0:q, full:N2], raw2[0:q, full:N2], ACT.Abs,
                                     accum_out=wsum[0:q, 3:4]).then_inc(a_abs, 1)

            def tanh(half, j, pair):
                n = HID[j]
                act.wait_ge(f_h.sem, f_h.done(half, j))
                if j >= 2:
                    act.wait_ge(f_a.sem, f_a.done(half, j - 2))
                ends(nc.scalar.activation(tanh_h[j % 2][0:n, :], h_ps[pair][0][0:n, :], ACT.Tanh,
                                          scale=scale[0:n, 6:7]), f_th)

            def split_gate(half, j):
                n = HID[j]
                act.wait_ge(f_g.sem, f_g.done(half, j))
                if half == H1:
                    act.wait_ge(f_y.sem, f_y.done(H0, j))
                ends(copy(g_hi[0:n, j, :], gate[j % 2][0:n, :]), f_gh)

            def split_last_gate(part):
                n, cols = HID[-1], PARTS[part]
                act.wait_ge(f_g.sem, f_g.part_done(H1, HC - 1, part))
                act.wait_ge(f_y.sem, f_y.done(H0, HC - 1))
                ends(copy(g_hi[0:n, HC - 1, cols], gate[(HC - 1) % 2][0:n, cols]), f_gh, 2)

            def normalise(half, s):
                act.wait_ge(f_nb.sem, f_nb.done(half, 1 if half == H0 else s // 2))
                row = row_tile(half, s)
                ends(nc.scalar.activation(x_all[:, row, :], r2(half, s), ACT.Identity,
                                          bias=shift2[:, row:row + 1], scale=rstd2[:, row:row + 1]), f_o)

            skip_first_chunk(act, a_x)
            for i in range(3):
                split_weight(i)
            k_parts(0)
            copy_v(0, 0)
            split_weight(3)
            act.wait_ge(v_kf.sem, v_kf.done(0))
            q_parts(0, 0, k_follows=False)
            q_high(0, 0)
            split_kt(0, 0)
            act.wait_ge(s_xt, 16)
            split_x(LOOP)
            split_weight(4)
            slot(0, 0, 0, first=True, x1=False)
            for i in (5, 6):
                split_weight(i)
            slot(0, 1, 0, x1=False)
            for i in (7, 8):
                split_weight(i)
            slot(0, 2, 0, x1=False)
            split_weight(9)
            slot(0, 3, 0, x1=False, sum_weights=True)
            sum_w2()
            with act.Fori(LOOP, C7 - 2 * LOOP + 1, 2 * LOOP) as c:
                for g in range(GROUPS):
                    slot(c, g, 1)
                for g in range(GROUPS):
                    slot(c + LOOP, g, 0)
            for g in range(GROUPS):
                if g < GROUPS - 1:
                    q_parts(C7, g + 1, k_follows=False)
                split_attn(*before(C7, g))
                if g < GROUPS - 1:
                    q_high(C7, g + 1)
                if g == 1:
                    act.wait_ge(g_q.sem, g_q.done(C7, 3))
                    act.wait_ge(v_scale, 3)
                if g:
                    tanh(H0, g - 1, 0)
                    split_gate(H0, g - 1)
                if g == 2:
                    split_x1(C6)
            tanh(H0, 3, 1)
            split_attn(C7, GROUPS - 1)
            split_gate(H0, 3)
            tanh(H0, 4, 0)
            split_gate(H0, 4)
            tanh(H0, 5, 1)
            split_x1(C7)
            split_gate(H0, 5)
            for j in range(HC):
                if j <= 1:
                    act.wait_ge(f_a.sem, f_a.done(H0, HC - 2 + j))
                if j in (1, HC - 1):
                    split_gate(H1, j - 1)
                tanh(H1, j, j % 2)
                if 1 < j < HC - 1:
                    split_gate(H1, j - 1)
            for part in range(2):
                split_last_gate(part)
            for s in range(TILES):
                normalise(H0, s)
            for s in (0, 1):
                normalise(H1, s)

        @block.vector
        def _(dve):
            start_at_one_round(dve, v_x, v_kr, v_qr, v_kf, v_kt, v_qf, v_pr, v_rden, v_de, v_at, v_st,
                               v_al, v_y, v_bs, v_mv, v_ve, v_x1, v_xl, f_a, f_g, f_gl, f_r, f_bs,
                               f_mv, f_ve, f_nb)

            def split_x(c):
                dve.wait_ge(a_x.sem, a_x.done(c))
                ends(nc.vector.tensor_tensor(xc_lo[:, :, :], xt_all[:, :, rows_of(c)],
                                             xc_hi[:, :, :].bitcast(F32), ALU.subtract), v_x)

            def split_weight(i):
                hi, lo = split_piece(i)
                dve.wait_ge(s_whi, i + 1)
                nc.vector.tensor_tensor(lo, raw_piece(i), hi.bitcast(F32), ALU.subtract).then_inc(v_wlo, 1)

            def rotate(c, u):
                b = PRODUCTS[u]
                if u == "k":
                    dve.wait_ge(p_k.sem, p_k.done(c))
                    dve.wait_ge(g_q.sem, g_q.done(c, -1))
                else:
                    dve.wait_ge(p_q.sem, p_q.done(c, u))
                    if u == 1:
                        dve.wait_ge(g_k.sem, g_k.done(c))
                    else:
                        dve.wait_ge(g_q.sem, g_q.done(c, u - 2))
                cos = rope[:, bass.ds(c * (ROPE_W // LOOP), HALF)]
                sin = rope[:, bass.ds(c * (ROPE_W // LOOP) + HALF, HD)]
                src = bank(u).rearrange("p (a e) -> p a e", e=HALF)
                nc.vector.tensor_tensor(rc[b][:, :].rearrange("p (a e) -> p a e", e=HALF), src,
                                        cos.unsqueeze(1).to_broadcast([P, 2 * REP, HALF]), ALU.mult)
                halves = "p (h t e) -> p h t e"
                sin = sin.rearrange("p (t e) -> p t e", t=2).unsqueeze(1)
                last = nc.vector.tensor_tensor(rs[b][:, :].rearrange(halves, t=2, e=HALF),
                                               bank(u).rearrange(halves, t=2, e=HALF)[:, :, ::-1, :],
                                               sin.to_broadcast([P, REP, 2, HALF]), ALU.mult)
                ends(last, v_kr if u == "k" else v_qr)

            def make_kf(c, par):
                dve.wait_ge(a_k.sem, a_k.done(c))
                dve.wait_ge(p_o.sem, p_o.done(c - 2 * LOOP, GROUPS - 1))
                ends(nc.vector.scalar_tensor_tensor(kf[par][:, :], k_exp[:, :], 1.0, k_relu[:, :],
                                                    ALU.min, ALU.add), v_kf)

            def split_kt(c, par):
                dve.wait_ge(a_kt.sem, a_kt.done(c))
                ends(nc.vector.tensor_tensor(kt_lo[par][:, :], turn_ps, kt_hi[par][:, :].bitcast(F32),
                                             ALU.subtract), v_kt)

            def make_qf(c, g):
                dve.wait_ge(a_q.sem, a_q.done(c, g))
                dve.wait_ge(p_o.sem, p_o.done(c, g - 2))
                ends(nc.vector.scalar_tensor_tensor(qf[g % 2][:, :], q_exp[:, :], 1.0, q_relu[:, :],
                                                    ALU.min, ALU.add), v_qf)

            def mask(c, g):
                dve.wait_ge(p_sc.sem, p_sc.done(c, g))
                dve.wait_ge(p_o.sem, p_o.done(c, g - 1))
                hq = "p (h q) -> p h q"
                ends(nc.vector.tensor_tensor(probs[:, :].rearrange(hq, h=REP),
                                             score_ps.rearrange(hq, h=REP),
                                             causal.unsqueeze(1).to_broadcast([P, REP, P]),
                                             ALU.mult), v_pr)

            def normalise(c, g, last_chunk=False):
                dve.wait_ge(p_o.sem, p_o.done(c, g))
                ends(nc.vector.tensor_scalar(den[:, :].rearrange("p (b h) -> p b h", b=2),
                                             o_ps[:, :, :, HD], DEN_EPS, None, ALU.add), v_de)
                if not last_chunk:
                    ends(nc.vector.tensor_tensor(state[:, g, 0:VW], upd_ps, state[:, g, 0:VW],
                                                 ALU.add), v_st)
                dve.wait_ge(v_de.sem, v_de.done(c, g))
                ends(nc.vector.reciprocal(rden[:, :], den[:, :]), v_rden)
                dve.wait_ge(v_rden.sem, v_rden.done(c, g))
                dve.wait_ge(p_at.sem, p_at.done(c, g - 1))
                rb = rden[:, :].rearrange("p (b h) -> p b h", b=2).unsqueeze(3).to_broadcast([P, 2, 2, HD])
                ends(nc.vector.tensor_tensor(attn[:, :].rearrange("p (b h d) -> p b h d", b=2, h=2),
                                             o_ps[:, :, :, 0:HD], rb, ALU.mult), v_at)

            def split_attn(c, g):
                dve.wait_ge(a_at.sem, a_at.done(c, g))
                ends(nc.vector.tensor_tensor(at_lo[:, :], at_ps, at_hi[:, :].bitcast(F32),
                                             ALU.subtract), v_al)

            def residual(c):
                dve.wait_ge(p_y.sem, p_y.done(c))
                ends(nc.vector.tensor_tensor(res[:, :].rearrange("p (a d) -> p a d", a=1),
                                             y_ps.rearrange("p (a d) -> p a d", a=1),
                                             x_all[:, bass.ds(c // LOOP, 1), :], ALU.add), v_y)

            def row_stats(c):
                row_sums(c)
                row_variance(c)

            def row_sums(c):
                dve.wait_ge(v_y.sem, v_y.done(c))
                ends(nc.vector.bn_stats(stats[:, :], res[:, :]), v_bs)

            def row_variance(c):
                dve.wait_ge(v_bs.sem, v_bs.done(c))
                ends(nc.vector.bn_aggr(mv[:, :], stats[:, :]), v_mv)
                dve.wait_ge(v_mv.sem, v_mv.done(c))
                ends(nc.vector.tensor_scalar(veps[:, :], mv[:, 1:2], LN_EPS, None, ALU.add), v_ve)

            def make_x1(c):
                dve.wait_ge(g_rs.sem, g_rs.done(c))
                dve.wait_ge(p_x1t.sem, p_x1t.done(c, -1))
                dve.wait_ge(g_x1.sem, g_x1.done(c, -1))
                ends(nc.vector.tensor_scalar(x1c[:, :], res[:, :], mv[:, 0:1], rstd[:, :],
                                             ALU.subtract, ALU.mult), v_x1)

            def split_x1(c):
                dve.wait_ge(a_x1.sem, a_x1.done(c))
                src = last_x1t_ps if c is C7 else at_ps[:, 0:DM]
                ends(nc.vector.tensor_tensor(x1t_lo[:, :, rows_of(c)],
                                             src.rearrange("p (k s) -> p k s", k=KT),
                                             x1t_hi[:, :, rows_of(c)].bitcast(F32), ALU.subtract), v_xl)

            def sum_w3():
                dve.wait_ge(s_w3, 16)
                dve.wait_ge(s_set, 2)
                nc.vector.tensor_reduce(wsum[:, 1:2], raw3, mybir.AxisListType.X, ALU.add,
                                        apply_absolute_value=True).then_inc(v_abs, 1)

            def slot(c, g, par, first=False, x1=True, weights=(), sum_weights=False):
                if g == 0 and not first:
                    split_x(c + LOOP)
                mask(c, g)
                if not first:
                    split_attn(*before(c, g))
                if g == 1 and x1:
                    make_x1(c - LOOP)
                make_qf(c, g + 1) if g < GROUPS - 1 else make_qf(c + LOOP, 0)
                for i in weights:
                    split_weight(i)
                if sum_weights:
                    sum_w3()
                for u in ROTATED_IN_SLOT[g]:
                    rotate(c + LOOP, u)
                if g == 1:
                    make_kf(c + LOOP, 1 - par)
                if g == 2:
                    split_kt(c + LOOP, 1 - par)
                normalise(c, g)
                if g == 0 and not first:
                    residual(c - LOOP)
                    row_stats(c - LOOP)
                if g == 1 and x1:
                    split_x1(c - LOOP)

            def ternary(n, w, t, s, below):
                dve.wait_ge(g_neg, n)
                nc.vector.scalar_tensor_tensor(t, w, scale[0:w.shape[0], 3 + s:4 + s], below,
                                               ALU.is_gt, ALU.subtract).then_inc(v_t, 1)

            def gate_low(half, j):
                n = HID[j]
                dve.wait_ge(f_gh.sem, f_gh.done(half, j))
                ends(nc.vector.tensor_tensor(g_lo[0:n, j, :], gate[j % 2][0:n, :],
                                             g_hi[0:n, j, :].bitcast(F32), ALU.subtract), f_gl)

            def last_gate_low(part):
                n, j, cols = HID[-1], HC - 1, PARTS[part]
                dve.wait_ge(f_gh.sem, f_gh.part_done(H1, j, part))
                ends(nc.vector.tensor_tensor(g_lo[0:n, j, cols], gate[j % 2][0:n, cols],
                                             g_hi[0:n, j, cols].bitcast(F32), ALU.subtract), f_gl, 2)

            def silu_part(half, j, pair):
                n = HID[j]
                dve.wait_ge(f_th.sem, f_th.done(half, j))
                if j:
                    dve.wait_ge(f_g.sem, f_g.done(half, j - 1))
                ends(nc.vector.scalar_tensor_tensor(gate_a[0:n, :], tanh_h[j % 2][0:n, :], 1.0,
                                                    h_ps[pair][0][0:n, :], ALU.add, ALU.mult), f_a)

            def make_gate(half, j, pair):
                n = HID[j]
                dve.wait_ge(f_a.sem, f_a.done(half, j))
                if j >= 2:
                    dve.wait_ge(f_gl.sem, f_gl.done(half, j - 2))
                ends(nc.vector.scalar_tensor_tensor(gate[j % 2][0:n, :], gate_a[0:n, :], scale[0:n, 7:8],
                                                    h_ps[pair][1][0:n, :], ALU.mult, ALU.mult), f_g)

            def last_silu_part(part):
                n, j, cols = HID[-1], HC - 1, PARTS[part]
                dve.wait_ge(f_th.sem, f_th.done(H1, j))
                dve.wait_ge(f_g.sem, f_g.done(H1, j - 1))
                ends(nc.vector.scalar_tensor_tensor(gate_a[0:n, cols], tanh_h[j % 2][0:n, cols], 1.0,
                                                    h_ps[j % 2][0][0:n, cols], ALU.add, ALU.mult), f_a, 2)

            def last_make_gate(part):
                n, j, cols = HID[-1], HC - 1, PARTS[part]
                dve.wait_ge(f_a.sem, f_a.part_done(H1, j, part))
                ends(nc.vector.scalar_tensor_tensor(gate[j % 2][0:n, cols], gate_a[0:n, cols],
                                                    scale[0:n, 7:8], h_ps[j % 2][1][0:n, cols],
                                                    ALU.mult, ALU.mult), f_g, 2)

            def residual2(half, tiles):
                for s in tiles:
                    row = row_tile(half, s)
                    ends(nc.vector.scalar_tensor_tensor(r2(half, s), y2_ps[s], scale[:, 2:3],
                                                        x_all[:, row, :], ALU.mult, ALU.add), f_r)

            def stats_of_tiles(half, tiles):
                for s in tiles:
                    dve.wait_ge(f_r.sem, f_r.done(half, s))
                    ends(nc.vector.bn_stats(stats2[:, row_tile(half, s), :], r2(half, s)), f_bs)

            def variance_of_tiles(half, tiles):
                means_of_tiles(half, tiles)
                add_eps(half, tiles)

            def means_of_tiles(half, tiles):
                for s in tiles:
                    dve.wait_ge(f_bs.sem, f_bs.done(half, s))
                    row = row_tile(half, s)
                    ends(nc.vector.bn_aggr(mv2[:, row, :], stats2[:, row, :]), f_mv)

            def add_eps(half, tiles):
                dve.wait_ge(f_mv.sem, f_mv.done(half, tiles[-1]))
                at = slice(row_tile(half, tiles[0]), row_tile(half, tiles[-1]) + 1)
                ends(nc.vector.tensor_scalar(veps2[:, at], mv2[:, at, 1], LN_EPS, None, ALU.add), f_ve)

            def shifts(half, tiles, parts):
                dve.wait_ge(f_rs.sem, f_rs.done(half, tiles[-1] // 2))
                at = slice(row_tile(half, tiles[0]), row_tile(half, tiles[-1]) + 1)
                last = nc.vector.scalar_tensor_tensor(shift2[:, at], mv2[:, at, 0], -1.0, rstd2[:, at],
                                                      ALU.mult, ALU.mult)
                last.then_inc(f_nb.sem, f_nb.step * parts)

            nc.vector.memset(ones[:, :], 1.0).then_inc(s_ones, 1)
            for par in range(2):
                nc.vector.memset(v1[par][:, :, HD:VS], 1.0)
            nc.vector.memset(state[:, :, :], 0.0)
            nc.vector.memset(neg_half[:, :], -0.5).then_inc(s_set, 1)
            nc.vector.memset(wsum[:, :], 0.0).then_inc(s_set, 1)
            skip_first_chunk(dve, v_x)
            split_weight(0)
            dve.wait_ge(s_const, 16)
            rotate(0, "k")
            rotate(0, 0)
            split_weight(1)
            make_kf(0, 0)
            rotate(0, 1)
            make_qf(0, 0)
            rotate(0, 2)
            split_kt(0, 0)
            dve.wait_ge(s_xt, 16)
            split_x(LOOP)
            rotate(0, 3)
            dve.wait_ge(s_rope, 16)
            slot(0, 0, 0, first=True, x1=False)
            split_weight(3)
            slot(0, 1, 0, x1=False, weights=(6,))
            split_weight(5)
            slot(0, 2, 0, x1=False)
            slot(0, 3, 0, x1=False, sum_weights=True)
            inv = 1.0 / (HIDDEN * DM)
            dve.wait_ge(p_sum, 1)
            nc.vector.tensor_scalar(scale[:, 0:3], sum_ps[:, 0:3], inv, None, ALU.mult).then_inc(v_scale, 1)
            dve.wait_ge(v_scale, 1)
            nc.vector.scalar_tensor_tensor(scale[:, 2:3], sum_ps[:, 3:4], inv, scale[:, 2:3],
                                           ALU.mult, ALU.add).then_inc(v_scale, 1)
            dve.wait_ge(v_scale, 2)
            nc.vector.tensor_scalar(scale[:, 3:6], scale[:, 0:3], 0.5, None, ALU.mult)
            nc.vector.tensor_scalar(scale[:, 8:11], scale[:, 0:3], -0.5, None, ALU.mult)
            nc.vector.tensor_scalar(scale[:, 6:7], scale[:, 0:1], 0.5, None, ALU.mult)
            nc.vector.tensor_scalar(scale[:, 7:8], scale[:, 0:1], scale[:, 1:2], 0.5, ALU.mult,
                                    ALU.mult).then_inc(v_scale, 1)
            dve.wait_ge(s_x, 16)
            with dve.Fori(LOOP, C7 - 2 * LOOP + 1, 2 * LOOP) as c:
                for g in range(GROUPS):
                    slot(c, g, 1)
                for g in range(GROUPS):
                    slot(c + LOOP, g, 0)
            full, at2 = (HC - 1) * DM, 2 * N1
            q = HID[-1]
            raw1_k, raw3_k, below1_k, below3_k = [a.rearrange("p (k n) -> p k n", k=KT)
                                                  for a in (raw1, raw3, below1, below3.bitcast(F32))]
            early, late = slice(0, 2 * HW), slice(2 * HW, HIDDEN)
            dve.wait_ge(p_q.sem, p_q.done(C7, 3))
            ternary(1, raw1_k[:, :, early], T1[:, :, early], 0, below1_k[:, :, early])
            for g in range(GROUPS):
                mask(C7, g)
                if g <= 1:
                    split_attn(*before(C7, g))
                if g < GROUPS - 1:
                    make_qf(C7, g + 1)
                if g >= 2:
                    split_attn(*before(C7, g))
                if g == 0:
                    ternary(1, raw1_k[:, :, late], T1[:, :, late], 0, below1_k[:, :, late])
                if g == 1:
                    row_stats(C6)
                if g:
                    silu_part(H0, g - 1, 0)
                    make_gate(H0, g - 1, 0)
                normalise(C7, g, last_chunk=True)
                if g == 0:
                    ternary(2, raw3_k[:, :, early], T3[:, :, early], 1, below3_k[:, :, early])
                    residual(C6)
                if g == 1:
                    make_x1(C6)
                    ternary(2, raw3_k[:, :, late], T3[:, :, late], 1, below3_k[:, :, late])
                if g == 2:
                    split_x1(C6)
            ternary(3, raw2[0:HW, 0:full], w_hi[0:HW, at2:at2 + full], 2, below2[0:HW, 0:full])
            ternary(4, raw2[0:q, full:N2], w_hi[0:q, at2 + full:at2 + N2], 2, below2[0:q, full:N2])
            silu_part(H0, 3, 1)
            split_attn(C7, GROUPS - 1)
            make_gate(H0, 3, 1)
            residual(C7)
            silu_part(H0, 4, 0)
            row_sums(C7)
            make_gate(H0, 4, 0)
            row_variance(C7)
            make_x1(C7)
            silu_part(H0, 5, 1)
            make_gate(H0, 5, 1)
            split_x1(C7)
            everything, first_two, last_two = range(TILES), (0, 1), (2, 3)
            for j in range(HC - 1):
                if j == 0:
                    dve.wait_ge(f_g.sem, f_g.done(H0, HC - 1))
                    dve.wait_ge(f_gl.sem, f_gl.done(H0, HC - 1))
                silu_part(H1, j, j % 2)
                make_gate(H1, j, j % 2)
                if j == 0:
                    dve.wait_ge(g_x1.sem, g_x1.done(C7))
                    dve.wait_ge(f_y.sem, f_y.done(H0, HC - 1))
                    residual2(H0, everything)
                if j == 1:
                    stats_of_tiles(H0, first_two)
                    variance_of_tiles(H0, first_two)
                if j == 4:
                    stats_of_tiles(H0, last_two)
            dve.wait_ge(f_gl.sem, f_gl.done(H1, HC - 3))
            gate_low(H1, HC - 2)
            last_silu_part(0)
            last_make_gate(0)
            last_silu_part(1)
            last_gate_low(0)
            last_make_gate(1)
            last_gate_low(1)
            variance_of_tiles(H0, last_two)
            dve.wait_ge(f_y.sem, f_y.part_done(H1, HC - 1, 0))
            residual2(H1, first_two)
            stats_of_tiles(H1, first_two)
            shifts(H0, everything, 2)
            dve.wait_ge(f_y.sem, f_y.part_done(H1, HC - 1, 1))
            residual2(H1, last_two)
            means_of_tiles(H1, first_two)
            stats_of_tiles(H1, (2,))
            add_eps(H1, first_two)
            stats_of_tiles(H1, (3,))
            means_of_tiles(H1, last_two)
            add_eps(H1, last_two)
            shifts(H1, first_two, 1)
            dve.wait_ge(f_rs.sem, f_rs.done(H1, 1))
            for s in last_two:
                row = row_tile(H1, s)
                nc.vector.tensor_scalar(x_all[:, row, :], r2(H1, s), mv2[:, row, 0:1],
                                        rstd2[:, row:row + 1], ALU.subtract, ALU.mult).then_inc(v_o, 1)

        @block.gpsimd
        def _(pool):
            start_at_one_round(pool, g_k, g_q, g_ql, g_rs, g_x1, f_rs)

            def split_weight(i):
                hi, lo = split_piece(i)
                pool.wait_ge(s_whi, i + 1)
                nc.gpsimd.tensor_tensor(lo, raw_piece(i), hi.bitcast(F32), ALU.subtract).then_inc(g_wlo, 1)

            def add_rotation(c, u):
                b = PRODUCTS[u]
                if u == "k":
                    pool.wait_ge(v_kr.sem, v_kr.done(c))
                    pool.wait_ge(a_k.sem, a_k.done(c, -1))
                    dst, st = k_rot, g_k
                else:
                    pool.wait_ge(v_qr.sem, v_qr.done(c, u))
                    pool.wait_ge(p_qt.sem, p_qt.done(c - LOOP, u))
                    dst, st = q_rot[u], g_q
                ends(nc.gpsimd.tensor_tensor(dst[:, :], rc[b][:, :], rs[b][:, :], ALU.add), st)

            def q_low(c, g):
                pool.wait_ge(a_qh.sem, a_qh.done(c, g))
                ends(nc.gpsimd.tensor_tensor(q_lo[:, :], qf[g % 2][:, :], q_hi[:, :].bitcast(F32),
                                             ALU.subtract), g_ql)

            def power(c):
                pool.wait_ge(v_ve.sem, v_ve.done(c))
                ends(nc.gpsimd.tensor_tensor(rstd[:, :], veps[:, :], neg_half[:, 0:1], ALU.pow), g_rs)

            def keep_x1(c):
                pool.wait_ge(v_x1.sem, v_x1.done(c))
                ends(nc.gpsimd.tensor_copy(x_all[:, bass.ds(c // LOOP, 1), :],
                                           x1c[:, :].rearrange("p (a d) -> p a d", a=1)), g_x1)

            def below(w, out, s, n):
                nc.gpsimd.tensor_scalar(out, w, scale[0:w.shape[0], 8 + s:9 + s], None,
                                        ALU.is_lt).then_inc(g_neg, 1)

            def gate_low(half, j):
                n = HID[j]
                pool.wait_ge(f_gh.sem, f_gh.done(half, j))
                ends(nc.gpsimd.tensor_tensor(g_lo[0:n, j, :], gate[j % 2][0:n, :],
                                             g_hi[0:n, j, :].bitcast(F32), ALU.subtract), f_gl)

            def slot(c, g, first=False, x1=True):
                q_low(c, g + 1) if g < GROUPS - 1 else q_low(c + LOOP, 0)
                for u in ROTATED_IN_SLOT[g]:
                    add_rotation(c + LOOP, u)
                if g == 0 and not first:
                    power(c - LOOP)
                if g == 1 and x1:
                    keep_x1(c - LOOP)

            pool.wait_ge(s_set, 1)
            add_rotation(0, "k")
            add_rotation(0, 0)
            split_weight(2)
            add_rotation(0, 1)
            q_low(0, 0)
            add_rotation(0, 2)
            add_rotation(0, 3)
            slot(0, 0, first=True)
            split_weight(4)
            slot(0, 1, x1=False)
            split_weight(7)
            slot(0, 2)
            split_weight(8)
            split_weight(9)
            slot(0, 3)
            pool.wait_ge(v_scale, 3)
            below(raw1, below1, 0, 1)
            with pool.Fori(LOOP, C7 - 2 * LOOP + 1, 2 * LOOP) as c:
                for g in range(GROUPS):
                    slot(c, g)
                for g in range(GROUPS):
                    slot(c + LOOP, g)
            pool.wait_ge(p_q.sem, p_q.done(C7, 3))
            below(raw3, below3, 1, 2)
            q_low(C7, 1)
            q_low(C7, 2)
            power(C6)
            pool.wait_ge(v_t, 2)
            full, q = (HC - 1) * DM, HID[-1]
            below(raw2[0:HW, 0:full], below2[0:HW, 0:full], 2, 3)
            keep_x1(C6)
            q_low(C7, 3)
            below(raw2[0:q, full:N2], below2[0:q, full:N2], 2, 4)
            for j in range(4):
                gate_low(H0, j)
            power(C7)
            gate_low(H0, 4)
            keep_x1(C7)
            gate_low(H0, 5)
            for j in range(4):
                gate_low(H1, j)
            pool.wait_ge(f_ve.sem, f_ve.done(H0, 1))
            nc.gpsimd.tensor_tensor(rstd2[:, 0:TILES], veps2[:, 0:TILES], neg_half[:, :],
                                    ALU.pow).then_inc(f_rs.sem, 2 * f_rs.step)
            for part in range(2):
                pool.wait_ge(f_ve.sem, f_ve.done(H1, part))
                at = slice(TILES + 2 * part, TILES + 2 * part + 2)
                ends(nc.gpsimd.tensor_tensor(rstd2[:, at], veps2[:, at], neg_half[:, 0:2], ALU.pow), f_rs)


def shape_tables():
    dim = np.arange(0, HD, 2, dtype=np.float32)
    inv_freq = (np.float32(1.0) / np.float32(ROPE_BASE) ** (dim / np.float32(HD))).astype(np.float32)
    angle = np.outer(np.arange(S, dtype=np.float32), inv_freq).astype(np.float32)
    cos, sin = np.cos(angle), np.sin(angle)
    by_chunk = lambda a: a.reshape(CHUNKS, P, -1).transpose(1, 0, 2).reshape(P, -1)
    causal = np.triu(np.ones((P, P), np.float32))
    rope = by_chunk(np.concatenate([cos, -sin, sin], 1))
    return np.ascontiguousarray(np.concatenate([causal, np.eye(P, dtype=np.float32), rope], 1))


def kernel(L0_attn_x, L0_attn_Wq, L0_attn_Wk, L0_attn_Wv, L0_attn_Wo, L0_ffn_w1, L0_ffn_w3, L0_ffn_w2):
    import concourse.bacc as bacc
    from concourse.bass_utils import run_bass_kernel_spmd

    lay = lambda a: np.ascontiguousarray(np.asarray(a))
    x = np.asarray(L0_attn_x)
    arrays = {
        "x_seq": lay(x[0]), "x_t": lay(x[0].T),
        "wq_t": lay(np.asarray(L0_attn_Wq).T), "wk_t": lay(np.asarray(L0_attn_Wk).T),
        "wv_t": lay(np.asarray(L0_attn_Wv).T), "wo_t": lay(np.asarray(L0_attn_Wo).T),
        "w1_t": lay(np.asarray(L0_ffn_w1).T), "w3_t": lay(np.asarray(L0_ffn_w3).T),
        "w2_t": lay(np.asarray(L0_ffn_w2).T), "tables": shape_tables(),
    }
    nc = bacc.Bacc("TRN2", target_bir_lowering=False, num_devices=1)
    args = [nc.dram_tensor(n, a.shape, mybir.dt.from_np(a.dtype), kind="ExternalInput").ap()
            for n, a in arrays.items()]
    out = nc.dram_tensor("out", (S, DM), F32, kind="ExternalOutput").ap()
    build(nc, *args, out)
    r = run_bass_kernel_spmd(nc, [arrays], core_ids=[0])
    return r.results[0]["out"].reshape(1, S, DM)
```
